# Optimizing a Trainium2 kernel written in Bass

```python
import numpy as np
import jax
import jax.numpy as jnp

def _softmax(x, axis=-1):
    return jax.nn.softmax(x, axis=axis)

def _gelu(x):
    return jax.nn.gelu(x, approximate=True)

def _silu(x):
    return jax.nn.silu(x)

def _sigmoid(x):
    return jax.nn.sigmoid(x)

def _layernorm(x, axis=-1, eps=1e-05):
    m = jnp.mean(x, axis=axis, keepdims=True)
    v = jnp.var(x, axis=axis, keepdims=True)
    return (x - m) / jnp.sqrt(v + eps)

def _scatter_add(tgt, idx, src, axis=0):
    return tgt.at[idx].add(src)

def _segment_sum(src, seg, n):
    return jax.ops.segment_sum(src, seg, n)
kernel_name = 'mk_recurrent_d1_jaxref_r8_f1a464'

def setup_inputs(seed: int=0):
    np.random.seed(seed)
    _w = jnp.asarray

    def _L0_attn_setup():
        import jax, jax.numpy as jnp
        import numpy as np
        HIDDEN = 256
        HEADS = 16
        HEAD_DIM = HIDDEN // HEADS
        NEG = -10000000000.0
        key = jax.random.key(seed)
        k1, k2, k3 = jax.random.split(key, 3)
        x = jax.random.normal(k1, (2, 256, HIDDEN), dtype=jnp.float32)
        w_qkv = jax.random.normal(k2, (HIDDEN, 3 * HIDDEN), dtype=jnp.float32) / np.sqrt(HIDDEN)
        w_out = jax.random.normal(k3, (HIDDEN, HIDDEN), dtype=jnp.float32) / np.sqrt(HIDDEN)
        return {'x': x, 'w_qkv': w_qkv, 'w_out': w_out}
    _L0_attn_in = _L0_attn_setup()

    def _L0_ffn_setup():
        import jax, jax.numpy as jnp
        import numpy as np
        N_BLOCKS = 6
        DIM = 256
        HIDDEN = 4 * DIM
        LN_EPS = 1e-05
        W_SCALE = 0.02

        def _block(x, w1, b1, w2, b2):
            h = jax.nn.gelu(jnp.einsum('bsd,hd->bsh', x, w1) + b1, approximate=False)
            return jnp.einsum('bsh,dh->bsd', h, w2) + b2 + x

        def _layernorm(x, g, b):
            mu = jnp.mean(x, axis=-1, keepdims=True)
            var = jnp.mean(jnp.square(x - mu), axis=-1, keepdims=True)
            return (x - mu) * jax.lax.rsqrt(var + LN_EPS) * g + b
        key = jax.random.key(seed)
        ks = jax.random.split(key, 4)
        x = jax.random.normal(ks[0], (4, 256, DIM), dtype=jnp.float32)
        W1 = jax.random.normal(ks[1], (N_BLOCKS, HIDDEN, DIM), dtype=jnp.float32) * W_SCALE
        B1 = jnp.zeros((N_BLOCKS, HIDDEN), dtype=jnp.float32)
        W2 = jax.random.normal(ks[2], (N_BLOCKS, DIM, HIDDEN), dtype=jnp.float32) * W_SCALE
        B2 = jnp.zeros((N_BLOCKS, DIM), dtype=jnp.float32)
        LN_G = jnp.ones((N_BLOCKS - 1, DIM), dtype=jnp.float32)
        LN_B = jnp.zeros((N_BLOCKS - 1, DIM), dtype=jnp.float32)
        return {'x': x, 'W1': W1, 'B1': B1, 'W2': W2, 'B2': B2, 'LN_G': LN_G, 'LN_B': LN_B}
    _L0_ffn_in = _L0_ffn_setup()
    _d = {'L0_attn_x': _L0_attn_in['x'], 'L0_attn_w_qkv': _L0_attn_in['w_qkv'], 'L0_attn_w_out': _L0_attn_in['w_out'], 'L0_ffn_W1': _L0_ffn_in['W1'], 'L0_ffn_B1': _L0_ffn_in['B1'], 'L0_ffn_W2': _L0_ffn_in['W2'], 'L0_ffn_B2': _L0_ffn_in['B2'], 'L0_ffn_LN_G': _L0_ffn_in['LN_G'], 'L0_ffn_LN_B': _L0_ffn_in['LN_B']}
    _x0 = _d['L0_attn_x']
    _d['L0_attn_x'] = jax.random.normal(jax.random.fold_in(jax.random.key(seed), 1), (4, 1024, 256), dtype=_x0.dtype)
    del _x0
    return _d

def reference(L0_attn_x, L0_attn_w_qkv, L0_attn_w_out, L0_ffn_W1, L0_ffn_B1, L0_ffn_W2, L0_ffn_B2, L0_ffn_LN_G, L0_ffn_LN_B):

    def _L0_attn_ref(x, w_qkv, w_out):
        import jax, jax.numpy as jnp
        import numpy as np
        HIDDEN = 256
        HEADS = 16
        HEAD_DIM = HIDDEN // HEADS
        NEG = -10000000000.0
        b, s, _ = x.shape
        qkv = x @ w_qkv
        qkv = qkv.reshape(b, s, 3, HEADS, HEAD_DIM)
        q, k, v = (qkv[:, :, 0], qkv[:, :, 1], qkv[:, :, 2])
        scale = jnp.sqrt(jnp.float32(HEAD_DIM)).astype(x.dtype)
        q = q / scale
        scores = jnp.einsum('bqhd,bkhd->bhqk', q, k)
        causal_mask = jnp.arange(s)[:, None] >= jnp.arange(s)[None, :]
        scores = jnp.where(causal_mask[None, None], scores, NEG)
        attn = jax.nn.softmax(scores, axis=-1)
        out = jnp.einsum('bhqk,bkhd->bqhd', attn, v).reshape(b, s, HIDDEN)
        return out @ w_out

    def _L0_ffn_ref(x, W1, B1, W2, B2, LN_G, LN_B):
        import jax, jax.numpy as jnp
        import numpy as np
        N_BLOCKS = 6
        DIM = 256
        HIDDEN = 4 * DIM
        LN_EPS = 1e-05
        W_SCALE = 0.02

        def _block(x, w1, b1, w2, b2):
            h = jax.nn.gelu(jnp.einsum('bsd,hd->bsh', x, w1) + b1, approximate=False)
            return jnp.einsum('bsh,dh->bsd', h, w2) + b2 + x

        def _layernorm(x, g, b):
            mu = jnp.mean(x, axis=-1, keepdims=True)
            var = jnp.mean(jnp.square(x - mu), axis=-1, keepdims=True)
            return (x - mu) * jax.lax.rsqrt(var + LN_EPS) * g + b
        for i in range(N_BLOCKS):
            x = _block(x, W1[i], B1[i], W2[i], B2[i])
            if i < N_BLOCKS - 1:
                x = _layernorm(x, LN_G[i], LN_B[i])
        return x
    x = L0_attn_x
    xn = _layernorm(x, axis=-1)
    s = _L0_attn_ref(xn, L0_attn_w_qkv, L0_attn_w_out)
    g = _silu(_L0_ffn_ref(xn, L0_ffn_W1, L0_ffn_B1, L0_ffn_W2, L0_ffn_B2, L0_ffn_LN_G, L0_ffn_LN_B))
    x = x + s * g
    return x

_drawn_inputs = setup_inputs


def setup_inputs(seed=0):
    import zlib

    import numpy as np

    out = dict(_drawn_inputs(seed))
    spreads = {'L0_ffn_B1': (0.0, 0.8),
     'L0_ffn_B2': (0.0, 0.363),
     'L0_ffn_LN_G': (1.0, 0.568),
     'L0_ffn_LN_B': (0.0, 0.443)}
    factors = {}
    for name, (base, spread) in spreads.items():
        noise = np.random.default_rng([zlib.crc32(name.encode()), seed]).standard_normal(out[name].shape)
        drawn = base * np.exp(spread * noise) if base else spread * noise
        out[name] = jnp.asarray(drawn.astype(out[name].dtype))
    for name, factor in factors.items():
        out[name] = (out[name] * factor).astype(out[name].dtype)
    return out
```

```python
from contextlib import ExitStack

import concourse.bass as bass
from concourse import mybir

F32 = mybir.dt.float32
F32R = mybir.dt.float32r
BF16 = mybir.dt.bfloat16
ALU = mybir.AluOpType
ACT = mybir.ActivationFunctionType
AX_X = mybir.AxisListType.X

P = 128
BATCH, SEQ, DIM = 4, 1024, 256
TOK = BATCH * SEQ
HEADS, HD = 16, 16
HALVES = DIM // P
GT = 512
TILES = GT // P
GROUPS = TOK // GT
PAIRS = GROUPS // 2
BLOCKS = 6
HID = 4 * DIM
CH = HID // P
EPS = 1e-5
HG = 4
QT = SEQ // P
BANK = 512
PARTS = 3
STACK = 6 * HD
ROWS = STACK + PARTS
SEARCH_SHARE = 0.85
NEG = -1.0e30


class Bufs:

    def __init__(self, nc, ctx):
        self.nc, self.ctx = nc, ctx

    def sb(self, name, shape, dt=F32):
        return self.ctx.enter_context(self.nc.sbuf_tensor(name, shape, dt))

    def ps(self, name, shape, dt=F32):
        return self.ctx.enter_context(self.nc.psum_tensor(name, shape, dt))

    def sem(self, name):
        return self.ctx.enter_context(self.nc.semaphore(name))


def wait_apart(eng, sem, value, passed):
    eng.wait_ge(sem, value)
    eng.sem_inc(passed, 1)


def project(nc, x, wqkv, scratch, keep):
    qd, kd, vd = scratch["q"], scratch["k"], scratch["v"]
    xth, xtl, xres, y, ident = keep["xth"], keep["xtl"], keep["xres"], keep["y"], keep["ident"]
    with ExitStack() as ctx:
        b = Bufs(nc, ctx)
        xin = [b.sb(f"p_xin{u}", [P, TILES, DIM]) for u in range(2)]
        w_raw = b.sb("p_w_raw", [P, HALVES, 3 * DIM])
        wh = b.sb("p_wh", [P, HALVES, 3 * DIM], F32R)
        wl = b.sb("p_wl", [P, HALVES, 3 * DIM], F32R)
        gth = [b.sb(f"p_gth{u}", [P, HALVES, GT], F32R) for u in range(2)]
        gtl = [b.sb(f"p_gtl{u}", [P, HALVES, GT], F32R) for u in range(2)]
        part = [b.sb(f"p_part{m}", [P, PARTS, GT], BF16) for m in range(4)]
        rest = [b.sb(f"p_rest{m}", [P, GT]) for m in range(2)]
        vout = [b.sb(f"p_vout{u}", [P, TILES, DIM]) for u in range(2)]
        stats = [b.sb(f"p_stats{u}", [P, TILES, 6]) for u in range(2)]
        mv = [b.sb(f"p_mv{u}", [P, TILES, 2]) for u in range(2)]
        var = [b.sb(f"p_var{u}", [P, TILES]) for u in range(2)]
        rstd = [b.sb(f"p_rstd{u}", [P, TILES]) for u in range(2)]
        tr_ps = b.ps("p_tr_ps", [P, HALVES, GT])
        qk_ps = [b.ps(f"p_qk_ps{u}", [P, GT]) for u in range(2)]
        v_ps = b.ps("p_v_ps", [P, TILES, DIM])

        w_loaded, w_high, w_split = b.sem("p_w_loaded"), b.sem("p_w_high"), b.sem("p_w_split")
        x_loaded = [b.sem(f"p_x_loaded{u}") for u in range(2)]
        stats_done, mean_done, var_ready = b.sem("p_stats_done"), b.sem("p_mean_done"), b.sem("p_var_ready")
        rstd_ready, normed = b.sem("p_rstd_ready"), b.sem("p_normed")
        xres_stored = [b.sem(f"p_xres_stored{u}") for u in range(2)]
        gt_stored = [b.sem(f"p_gt_stored{u}") for u in range(2)]
        transposed, high_done, low_done = b.sem("p_transposed"), b.sem("p_high_done"), b.sem("p_low_done")
        qk_done, part0_done, rest_done = b.sem("p_qk_done"), b.sem("p_part0_done"), b.sem("p_rest_done")
        part1_done, part2_done = b.sem("p_part1_done"), b.sem("p_part2_done")
        part_stored = [b.sem(f"p_part_stored{m}") for m in range(4)]
        v_done, v_copied = b.sem("p_v_done"), b.sem("p_v_copied")
        v_stored = [b.sem(f"p_v_stored{u}") for u in range(2)]
        ident_ready = b.sem("p_ident_ready")
        half_ready, passed = b.sem("p_half_ready"), b.sem("p_passed")

        block = ctx.enter_context(nc.Block())

        def pairs(eng, body):
            with eng.Fori(0, PAIRS - 1) as p:
                body(p, False)
            body(PAIRS - 1, True)

        @block.sync
        def _(sp):
            sp.dma_start(w_raw[:], wqkv.rearrange("(c p) n -> p c n", p=P)).then_inc(w_loaded, 16)
            xg = x.rearrange("(g j p) d -> g p j d", p=P, j=TILES)

            def load_x(g, u):
                sp.dma_start(xin[u][:], xg[g]).then_inc(x_loaded[u], 16)

            load_x(0, 0)
            load_x(1, 1)

            def body(p, last):
                for u in range(2):
                    g = 2 * p + u
                    sp.wait_ge(normed, g + 3)
                    sp.dma_start(xres[:, bass.ds(TILES * g, TILES), :], y[u][:]).then_inc(xres_stored[u], 16)
                    if not last:
                        load_x(g + 2, u)
                    sp.wait_ge(low_done, g + 2)
                    sp.dma_start(xth[:, :, bass.ds(GT * g, GT)].bitcast(F32), gth[u][:].bitcast(F32)).then_inc(gt_stored[u], 16)
                    sp.dma_start(xtl[:, :, bass.ds(GT * g, GT)].bitcast(F32), gtl[u][:].bitcast(F32)).then_inc(gt_stored[u], 16)

            pairs(sp, body)
            for u in range(2):
                sp.wait_ge(xres_stored[u], 16 * (PAIRS + 1))
                sp.wait_ge(gt_stored[u], 32 * (PAIRS + 1))

        @block.gpsimd
        def _(pool):
            nc.gpsimd.memset(ident[:], 0.0).then_inc(ident_ready, 1)
            nc.gpsimd.memset(keep["mhalf"][:], -0.5).then_inc(half_ready, 1)
            pool.wait_ge(ident_ready, 1)
            nc.gpsimd.affine_select(out=ident[:], in_=ident[:], compare_op=ALU.not_equal, fill=1.0,
                                    base=0, pattern=[[-1, P]], channel_multiplier=1).then_inc(ident_ready, 1)
            pool.wait_ge(half_ready, 1)

            with pool.Fori(0, PAIRS) as p:
                for u in range(2):
                    pool.wait_ge(var_ready, 2 * p + u + 1)
                    nc.gpsimd.tensor_tensor(rstd[u][:], var[u][:], keep["mhalf"][:], ALU.pow).then_inc(rstd_ready, 1)

        @block.vector
        def _(dve):
            dve.sem_inc(normed, 2)
            dve.sem_inc(low_done, 1)
            dve.sem_inc(rest_done, 2)
            dve.sem_inc(part2_done, 2)
            dve.wait_ge(w_loaded, 16)
            nc.vector.tensor_copy(wh[:], w_raw[:]).then_inc(w_high, 1)
            dve.wait_ge(w_high, 1)
            nc.vector.tensor_tensor(wl[:], w_raw[:], wh[:].bitcast(F32), ALU.subtract).then_inc(w_split, 1)

            def norm(g, u, n):
                dve.wait_ge(x_loaded[u], 16 * n)
                for j in range(TILES):
                    i = nc.vector.bn_stats(stats[u][:, j, :], xin[u][:, j, :])
                i.then_inc(stats_done, 1)
                wait_apart(dve, stats_done, g + 1, passed)
                for j in range(TILES):
                    i = nc.vector.bn_aggr(mv[u][:, j, :], stats[u][:, j, :])
                i.then_inc(mean_done, 1)
                dve.wait_ge(mean_done, g + 1)
                nc.vector.tensor_scalar(var[u][:], mv[u][:, :, 1], EPS, None, ALU.add).then_inc(var_ready, 1)
                dve.wait_ge(transposed, g + 1)
                dve.wait_ge(xres_stored[u], 16 * n)
                dve.wait_ge(rstd_ready, g + 1)
                for j in range(TILES):
                    i = nc.vector.tensor_scalar(y[u][:, j, :], xin[u][:, j, :], mv[u][:, j, 0:1],
                                                rstd[u][:, j:j + 1], ALU.subtract, ALU.mult)
                i.then_inc(normed, 1)

            def low(g, u):
                dve.wait_ge(high_done, g + 1)
                nc.vector.tensor_tensor(gtl[u][:], tr_ps[:], gth[u][:].bitcast(F32), ALU.subtract).then_inc(low_done, 1)

            def split_rest(g, m):
                dve.wait_ge(part0_done, 4 * g + m + 1)
                dve.wait_ge(part2_done, 4 * g + m + 1)
                nc.vector.scalar_tensor_tensor(rest[m % 2][:], qk_ps[m % 2][:], 0.25 if m < 2 else 1.0,
                                               part[m][:, 0, :], ALU.mult, ALU.subtract).then_inc(rest_done, 1)

            def split_last(g, m):
                dve.wait_ge(part1_done, 4 * g + m + 1)
                nc.vector.tensor_tensor(part[m][:, 2, :], rest[m % 2][:], part[m][:, 1, :],
                                        ALU.subtract).then_inc(part2_done, 1)

            norm(0, 0, 1)
            low(0, 0)

            def body(p, last):
                for u in range(2):
                    g = 2 * p + u
                    more = not (last and u == 1)
                    if more:
                        norm(g + 1, 1 - u, p + 1 + u)
                    split_rest(g, 0)
                    split_rest(g, 1)
                    split_last(g, 0)
                    split_last(g, 1)
                    split_rest(g, 2)
                    split_rest(g, 3)
                    split_last(g, 2)
                    if more:
                        low(g + 1, 1 - u)
                    split_last(g, 3)

            pairs(dve, body)

        @block.scalar
        def _(act):
            act.sem_inc(v_copied, 1)
            for u in range(2):
                act.sem_inc(xres_stored[u], 16)
                act.sem_inc(gt_stored[u], 32)
                act.sem_inc(v_stored[u], 16)
            for m in range(4):
                act.sem_inc(part_stored[m], 16)

            def high(g, u, n):
                act.wait_ge(transposed, g + 3)
                act.wait_ge(v_done, g + 1)
                act.wait_ge(gt_stored[u], 32 * n)
                nc.scalar.activation(gth[u][:], tr_ps[:], ACT.Copy).then_inc(high_done, 1)

            def part0(g, m):
                act.wait_ge(qk_done, 4 * g + m + 1)
                act.wait_ge(part_stored[m], 16 * g + 16)
                nc.scalar.activation(part[m][:, 0, :], qk_ps[m % 2][:], ACT.Copy,
                                     scale=0.25 if m < 2 else 1.0).then_inc(part0_done, 1)

            def part1(g, m):
                act.wait_ge(rest_done, 4 * g + m + 3)
                nc.scalar.activation(part[m][:, 1, :], rest[m % 2][:], ACT.Copy).then_inc(part1_done, 1)

            def store(g, m):
                act.wait_ge(part2_done, 4 * g + m + 3)
                rows = (qd if m < 2 else kd)[P * (m % 2):P * (m % 2) + P]
                act.dma_start(rows[:, :, bass.ds(GT * g, GT)], part[m][:]).then_inc(part_stored[m], 16)

            high(0, 0, 1)

            def body(p, last):
                for u in range(2):
                    g = 2 * p + u
                    part0(g, 0)
                    part0(g, 1)
                    part1(g, 0)
                    part1(g, 1)
                    part0(g, 2)
                    part0(g, 3)
                    part1(g, 2)
                    store(g, 0)
                    if not (last and u == 1):
                        high(g + 1, 1 - u, p + 1 + u)
                    part1(g, 3)
                    store(g, 1)
                    store(g, 2)
                    act.wait_ge(v_done, g + 3)
                    act.wait_ge(v_stored[u], 16 * p + 16)
                    nc.scalar.activation(vout[u][:], v_ps[:], ACT.Copy).then_inc(v_copied, 1)
                    store(g, 3)
                    act.wait_ge(v_copied, g + 2)
                    act.dma_start(vd.rearrange("(g j p) d -> g p j d", p=P, j=TILES)[g], vout[u][:]).then_inc(v_stored[u], 16)

            pairs(act, body)
            for m in range(4):
                act.wait_ge(part_stored[m], 16 * (GROUPS + 1))
            for u in range(2):
                act.wait_ge(v_stored[u], 16 * (PAIRS + 1))

        @block.tensor
        def _(pe):
            pe.sem_inc(transposed, 2)
            pe.sem_inc(v_done, 2)
            pe.wait_ge(ident_ready, 2)

            def transpose(g, u):
                pe.wait_ge(normed, g + 3)
                pe.wait_ge(low_done, g + 1)
                for c in range(HALVES):
                    for j in range(TILES):
                        i = nc.tensor.transpose(tr_ps[:, c, j * P:(j + 1) * P], y[u][:, j, c * P:(c + 1) * P], ident[:])
                i.then_inc(transposed, 1)

            transpose(0, 0)
            pe.wait_ge(w_split, 1)

            def body(p, last):
                for u in range(2):
                    g = 2 * p + u
                    pe.wait_ge(low_done, g + 2)
                    for m in range(4):
                        pe.wait_ge(rest_done, 4 * g + m + 1)
                        cols = slice(P * m, P * m + P)
                        for c in range(HALVES):
                            for w, t in ((wh, gth), (wh, gtl), (wl, gth)):
                                i = nc.tensor.matmul(qk_ps[m % 2][:], w[:, c, cols], t[u][:, c, :],
                                                     start=(c == 0 and w is wh and t is gth),
                                                     stop=(c == HALVES - 1 and w is wl))
                        i.then_inc(qk_done, 1)
                    if not (last and u == 1):
                        transpose(g + 1, 1 - u)
                    pe.wait_ge(v_copied, g + 1)
                    for j in range(TILES):
                        for c in range(HALVES):
                            for t, w in ((gth, wh), (gth, wl), (gtl, wh)):
                                first = c == 0 and t is gth and w is wh
                                i = nc.tensor.matmul(v_ps[:, j, :], t[u][:, c, j * P:(j + 1) * P],
                                                     w[:, c, 2 * DIM:3 * DIM], start=(first and j % 2 == 0),
                                                     stop=(c == HALVES - 1 and t is gtl), skip_group_check=True)
                    i.then_inc(v_done, 1)

            pairs(pe, body)


def mlp(nc, w1t, w2t, b1, b2, ln_g, ln_b, scratch, keep):
    fd = scratch["f"]
    xth, xtl, xres, y, ident = keep["xth"], keep["xtl"], keep["xres"], keep["y"], keep["ident"]
    SLOTS = BLOCKS * GROUPS
    with ExitStack() as ctx:
        b = Bufs(nc, ctx)
        raw1 = [b.sb(f"m_raw1{u}", [P, HALVES, P]) for u in range(2)]
        raw2 = [b.sb(f"m_raw2{u}", [P, DIM]) for u in range(2)]
        w1h = [b.sb(f"m_w1h{u}", [P, HALVES, HID], F32R) for u in range(2)]
        w1l = [b.sb(f"m_w1l{u}", [P, HALVES, HID], F32R) for u in range(2)]
        w2h = [b.sb(f"m_w2h{u}", [P, CH, DIM], F32R) for u in range(2)]
        w2l = [b.sb(f"m_w2l{u}", [P, CH, DIM], F32R) for u in range(2)]
        b1s = [b.sb(f"m_b1s{u}", [P, CH]) for u in range(2)]
        b2s = [b.sb(f"m_b2s{u}", [P, 1, DIM]) for u in range(2)]
        lng = [b.sb(f"m_lng{u}", [P, DIM]) for u in range(2)]
        lnb = [b.sb(f"m_lnb{u}", [P, DIM]) for u in range(2)]
        hid = [b.sb(f"m_hid{k}", [P, GT]) for k in range(2)]
        hidh = [b.sb(f"m_hidh{k}", [P, GT], F32R) for k in range(4)]
        hidl = [b.sb(f"m_hidl{k}", [P, GT], F32R) for k in range(4)]
        stats = b.sb("m_stats", [P, TILES, 6])
        mv = b.sb("m_mv", [P, TILES, 2])
        var = b.sb("m_var", [P, TILES])
        rstd = b.sb("m_rstd", [P, TILES])
        h_ps = [b.ps(f"m_h_ps{k}", [P, GT]) for k in range(2)]
        y_ps = [b.ps(f"m_y_ps{u}", [P, TILES, DIM]) for u in range(2)]
        tr_ps = b.ps("m_tr_ps", [P, HALVES, GT])

        raw_loaded = [b.sem(f"m_raw_loaded{u}") for u in range(2)]
        bias_loaded = [b.sem(f"m_bias_loaded{u}") for u in range(2)]
        ln_loaded = [b.sem(f"m_ln_loaded{u}") for u in range(2)]
        w_high, w_split = b.sem("m_w_high"), b.sem("m_w_split")
        w1_done, gelu_done, low_done = b.sem("m_w1_done"), b.sem("m_gelu_done"), b.sem("m_low_done")
        w2_done, y_added, b2_added = b.sem("m_w2_done"), b.sem("m_y_added"), b.sem("m_b2_added")
        stats_done, mean_done, var_ready = b.sem("m_stats_done"), b.sem("m_mean_done"), b.sem("m_var_ready")
        rstd_ready, scaled, x_ready = b.sem("m_rstd_ready"), b.sem("m_scaled"), b.sem("m_x_ready")
        transposed, xth_done, xtl_done = b.sem("m_transposed"), b.sem("m_xth_done"), b.sem("m_xtl_done")
        xres_done, passed = b.sem("m_xres_done"), b.sem("m_passed")
        f_stored = [b.sem(f"m_f_stored{u}") for u in range(2)]

        block = ctx.enter_context(nc.Block())

        class Slot:

            def __init__(s, i, gp, u, par, nth, kind, first):
                s.i, s.gp, s.u, s.par, s.nth, s.kind = i, gp, u, par, nth, kind
                s.g = 2 * gp + u
                s.t = GROUPS * i + s.g
                s.seam = first and u == 0
                s.start = kind == "first" and s.seam
                s.second = kind == "first" and first and u == 1
                s.epar = 1 - par if s.seam else par
                s.enth = nth - (1 - par) if s.seam else nth
                s.eg = GROUPS - 1 if s.seam else s.g - 1
                s.first = first
                s.final = kind == "last" and not s.seam
                s.more = kind != "last"

        def sweep(eng, slot, begin=None):
            def one(i, par, nth, kind):
                if begin:
                    begin(i, par, nth, kind)
                for u in range(2):
                    slot(Slot(i, 0, u, par, nth, kind, True))
                with eng.Fori(1, PAIRS) as gp:
                    for u in range(2):
                        slot(Slot(i, gp, u, par, nth, kind, False))

            one(0, 0, 1, "first")
            with eng.Fori(0, (BLOCKS - 2) // 2) as q:
                one(2 * q + 1, 1, q + 1, "middle")
                one(2 * q + 2, 0, q + 2, "middle")
            one(BLOCKS - 1, 1, BLOCKS // 2, "last")

        @block.sync
        def _(sp):
            w1v = w1t.rearrange("i (c p) h -> i p c h", p=P)

            def load_raw(i, g, u):
                sp.dma_start(raw1[u][:], w1v[i][:, :, bass.ds(P * g, P)]).then_inc(raw_loaded[u], 16)
                sp.dma_start(raw2[u][:], w2t[i, bass.ds(P * g, P), :]).then_inc(raw_loaded[u], 16)

            def load_bias(i, par):
                sp.dma_start(b1s[par][:], b1[i]).then_inc(bias_loaded[par], 16)
                sp.dma_start(b2s[par][:, 0, :], b2[bass.ds(i, 1), :].broadcast_to([P, DIM])).then_inc(bias_loaded[par], 16)

            for g in range(GROUPS):
                if g >= 2:
                    sp.wait_ge(w_split, g - 1)
                load_raw(0, g, g % 2)
                if g == 0:
                    load_bias(0, 0)

            def begin(i, par, nth, kind):
                if kind == "last":
                    return
                if kind == "middle":
                    sp.wait_ge(x_ready, GROUPS * i - 7)
                sp.dma_start(lng[par][:], ln_g[bass.ds(i, 1), :].broadcast_to([P, DIM])).then_inc(ln_loaded[par], 16)
                sp.dma_start(lnb[par][:], ln_b[bass.ds(i, 1), :].broadcast_to([P, DIM])).then_inc(ln_loaded[par], 16)

            def slot(s):
                if s.more:
                    piece = GROUPS * (s.i + 1) + s.g
                    sp.wait_ge(w_split, piece - 1)
                    load_raw(s.i + 1, s.g, s.u)
                    if s.second or (s.kind == "middle" and s.first and s.u == 1):
                        if s.kind == "middle":
                            sp.wait_ge(b2_added, GROUPS * s.i)
                        load_bias(s.i + 1, 1 - s.par)
                if s.final:
                    store_f(s.t, s.eg, s.epar, (s.u + 1) % 2)

            def store_f(t, eg, epar, yu):
                sp.wait_ge(b2_added, t)
                sp.dma_start(fd.rearrange("(g j p) d -> g p j d", p=P, j=TILES)[eg], y[yu][:]).then_inc(f_stored[yu], 16)

            sweep(sp, slot, begin)
            store_f(SLOTS, GROUPS - 1, 1, 1)
            for u in range(2):
                sp.wait_ge(f_stored[u], 16 * (PAIRS + 1))

        @block.gpsimd
        def _(pool):
            def slot(s):
                if not s.start:
                    add_b2(s.t, s.epar, 1 - s.u)
                    if not s.final:
                        pool.wait_ge(var_ready, s.t)
                        nc.gpsimd.tensor_tensor(rstd[:], var[:], keep["mhalf"][:], ALU.pow).then_inc(rstd_ready, 1)

            def add_b2(t, epar, yu):
                pool.wait_ge(y_added, t + 2)
                nc.gpsimd.tensor_tensor(y[yu][:], y[yu][:], b2s[epar][:].broadcast_to([P, TILES, DIM]),
                                        ALU.add).then_inc(b2_added, 1)

            def begin(i, par, nth, kind):
                pool.wait_ge(bias_loaded[par], 32 * nth)

            sweep(pool, slot, begin)
            add_b2(SLOTS, 1, 1)

        @block.scalar
        def _(act):
            act.preload_act_table(ACT.Gelu)
            act.sem_inc(gelu_done, 2)
            act.sem_inc(xres_done, 1)
            for u in range(2):
                act.sem_inc(f_stored[u], 16)

            def begin(i, par, nth, kind):
                act.wait_ge(bias_loaded[par], 32 * nth)

            def slot(s):
                for k in range(CH):
                    n = CH * s.t + k
                    act.wait_ge(w1_done, n + 1)
                    act.wait_ge(low_done, n + 1)
                    nc.scalar.activation(hid[k % 2][:], h_ps[k % 2][:], ACT.Gelu, bias=b1s[s.par][:, k:k + 1])
                    act.wait_ge(w2_done, n + 1)
                    nc.scalar.activation(hidh[k % 4][:], h_ps[k % 2][:], ACT.Gelu, bias=b1s[s.par][:, k:k + 1]).then_inc(gelu_done, 1)
                if s.start or s.final:
                    return
                act.wait_ge(transposed, s.t + 1)
                nc.scalar.activation(xth[:, :, bass.ds(GT * s.eg, GT)], tr_ps[:], ACT.Copy).then_inc(xth_done, 1)
                act.wait_ge(x_ready, s.t + 1)
                nc.scalar.activation(xres[:, bass.ds(TILES * s.eg, TILES), :], y[1 - s.u][:], ACT.Copy).then_inc(xres_done, 1)

            sweep(act, slot, begin)

        @block.vector
        def _(dve):
            dve.sem_inc(low_done, 2)
            dve.sem_inc(y_added, 2)
            dve.sem_inc(x_ready, 1)

            def split_weights(i, g, u, par, nth):
                piece = GROUPS * i + g
                cols = bass.ds(P * g, P)
                dve.wait_ge(raw_loaded[u], 32 * nth)
                nc.vector.tensor_copy(w1h[par][:, :, cols], raw1[u][:])
                nc.vector.tensor_copy(w2h[par][:, bass.ds(g, 1), :].squeeze(1), raw2[u][:]).then_inc(w_high, 1)
                dve.wait_ge(w_high, piece + 1)
                nc.vector.tensor_tensor(w1l[par][:, :, cols], raw1[u][:], w1h[par][:, :, cols].bitcast(F32), ALU.subtract)
                nc.vector.tensor_tensor(w2l[par][:, bass.ds(g, 1), :].squeeze(1), raw2[u][:], w2h[par][:, bass.ds(g, 1), :].squeeze(1).bitcast(F32),
                                        ALU.subtract).then_inc(w_split, 1)

            for g in range(GROUPS):
                split_weights(0, g, g % 2, 0, g // 2 + 1)

            def add_y(t, eg, yu):
                dve.wait_ge(w2_done, CH * t + 4)
                nc.vector.tensor_tensor(y[yu][:], y_ps[yu][:], xres[:, bass.ds(TILES * eg, TILES), :],
                                        ALU.add).then_inc(y_added, 1)

            def slot(s):
                epilogue = not (s.start or s.final)
                if not s.start:
                    if s.kind == "last" and not s.first:
                        dve.wait_ge(f_stored[1 - s.u], 16 * s.gp + 16 * s.u)
                        dve.wait_ge(transposed, GROUPS * (BLOCKS - 1) + 1)
                        dve.wait_ge(xres_done, GROUPS * (BLOCKS - 1) + 1)
                    elif not s.second:
                        dve.wait_ge(transposed, s.t - 1)
                        dve.wait_ge(xres_done, s.t - 1)
                    add_y(s.t, s.eg, 1 - s.u)
                yy = y[1 - s.u]
                for k in range(CH):
                    n = CH * s.t + k
                    dve.wait_ge(gelu_done, n + 3)
                    nc.vector.tensor_tensor(hidl[k % 4][:], hid[k % 2][:], hidh[k % 4][:].bitcast(F32),
                                            ALU.subtract).then_inc(low_done, 1)
                    if k == 1 and epilogue:
                        dve.wait_ge(b2_added, s.t)
                        for j in range(TILES):
                            i = nc.vector.bn_stats(stats[:, j, :], yy[:, j, :])
                        i.then_inc(stats_done, 1)
                    if k == 2 and epilogue:
                        wait_apart(dve, stats_done, s.t, passed)
                        for j in range(TILES):
                            i = nc.vector.bn_aggr(mv[:, j, :], stats[:, j, :])
                        i.then_inc(mean_done, 1)
                    if k == 3 and epilogue:
                        dve.wait_ge(mean_done, s.t)
                        nc.vector.tensor_scalar(var[:], mv[:, :, 1], EPS, None, ALU.add).then_inc(var_ready, 1)
                        dve.wait_ge(ln_loaded[s.epar], 32 * s.enth)
                        for j in range(TILES):
                            i = nc.vector.scalar_tensor_tensor(yy[:, j, :], yy[:, j, :], mv[:, j, 0:1], lng[s.epar][:],
                                                               ALU.subtract, ALU.mult)
                        i.then_inc(scaled, 1)
                    if k == 4 and s.more:
                        split_weights(s.i + 1, s.g, s.u, 1 - s.par, 4 * (s.i + 1) + s.gp + 1)
                    if k == 5 and epilogue:
                        dve.wait_ge(scaled, s.t)
                        dve.wait_ge(rstd_ready, s.t)
                        for j in range(TILES):
                            i = nc.vector.scalar_tensor_tensor(yy[:, j, :], yy[:, j, :], rstd[:, j:j + 1], lnb[s.epar][:],
                                                               ALU.mult, ALU.add)
                        i.then_inc(x_ready, 1)
                if epilogue:
                    cols = bass.ds(GT * s.eg, GT)
                    dve.wait_ge(xth_done, s.t)
                    nc.vector.tensor_tensor(xtl[:, :, cols], tr_ps[:], xth[:, :, cols].bitcast(F32),
                                            ALU.subtract).then_inc(xtl_done, 1)

            sweep(dve, slot)
            dve.wait_ge(f_stored[1], 16 * PAIRS)
            add_y(SLOTS, GROUPS - 1, 1)

        @block.tensor
        def _(pe):
            pe.sem_inc(w2_done, 4)
            pe.sem_inc(transposed, 1)

            def begin(i, par, nth, kind):
                pe.wait_ge(w_split, GROUPS * (i + 1))

            def slot(s):
                tokens = bass.ds(GT * s.g, GT)

                def up(k):
                    pe.wait_ge(gelu_done, CH * s.t + k + 1)
                    for c in range(HALVES):
                        for w, x in ((w1h, xth), (w1h, xtl), (w1l, xth)):
                            i = nc.tensor.matmul(h_ps[k % 2][:], w[s.par][:, c, k * P:(k + 1) * P], x[:, c, tokens],
                                                 start=(c == 0 and w is w1h and x is xth), stop=(c == HALVES - 1 and w is w1l))
                    i.then_inc(w1_done, 1)

                def down(k):
                    pe.wait_ge(low_done, CH * s.t + k + 3)
                    if k == 0:
                        pe.wait_ge(y_added, s.t + 1)
                    for j in range(TILES):
                        for h, w in ((hidh, w2h), (hidh, w2l), (hidl, w2h)):
                            i = nc.tensor.matmul(y_ps[s.u][:, j, :], h[k % 4][:, j * P:(j + 1) * P], w[s.par][:, k, :],
                                                 start=(k == 0 and j % 2 == 0 and h is hidh and w is w2h),
                                                 stop=(k == CH - 1 and h is hidl), skip_group_check=True)
                    i.then_inc(w2_done, 1)

                if s.kind != "first":
                    pe.wait_ge(xtl_done, s.t - 7)
                for k in range(CH):
                    up(k)
                    if k >= 2:
                        down(k - 2)
                if not (s.start or s.final):
                    pe.wait_ge(x_ready, s.t + 1)
                    if not s.second:
                        pe.wait_ge(xtl_done, s.t - 1)
                    for c in range(HALVES):
                        for j in range(TILES):
                            i = nc.tensor.transpose(tr_ps[:, c, j * P:(j + 1) * P],
                                                    y[1 - s.u][:, j, c * P:(c + 1) * P], ident[:])
                    i.then_inc(transposed, 1)
                down(CH - 2)
                down(CH - 1)

            sweep(pe, slot, begin)


def max_pieces():
    return [(j, qt, half) for j in range(HG) for qt in range(QT) for half in range(1 + qt // HG)]


def score_units():
    per = {kt: 1 if kt < 4 else 2 if kt < 6 else HG for kt in range(QT)}
    return [(kt, j, per[kt]) for kt in range(QT) for j in range(0, HG, per[kt])]


def schedule_pieces():
    pieces = max_pieces()
    cost = [min(P * (qt + 1) - BANK * half, BANK) + 60 for _, qt, half in pieces]
    work = [(SEQ - P * kt) * heads for kt, _, heads in score_units()]
    until = sum(work) * SEARCH_SHARE
    counts, done, spent, n = [], 0, 0, 0
    for w in work:
        done += w
        k = 0
        while n < len(pieces) and spent + cost[n] / 2 <= sum(cost) * done / until:
            spent += cost[n]
            n += 1
            k += 1
        counts.append(k)
    assert n == len(pieces)
    return counts


def attend(nc, scratch):
    qd, kd, vd, od = scratch["q"], scratch["k"], scratch["v"], scratch["o"]
    N_GROUPS = BATCH * HG
    PIECES = max_pieces()
    NP = len(PIECES)
    AFTER = schedule_pieces()
    UNITS = score_units()
    NU = len(UNITS)
    LAST_OF = {kt: max(n for n, unit in enumerate(UNITS) if unit[0] == kt) for kt in range(QT)}
    FIRST_OF = {kt: min(n for n, unit in enumerate(UNITS) if unit[0] == kt) for kt in range(QT)}
    with ExitStack() as ctx:
        b = Bufs(nc, ctx)
        qs = [b.sb(f"a_qs{s}", [P, HG, SEQ], BF16) for s in range(HG)]
        ks = [b.sb(f"a_ks{s}", [P, HG, SEQ], BF16) for s in range(HG)]
        v_raw = [b.sb(f"a_v_raw{u}", [P, QT, HG * HD]) for u in range(2)]
        va = [b.sb(f"a_va{u}", [P, QT, HG, 2 * HD]) for u in range(2)]
        prob = [b.sb(f"a_prob{u}", [P, HG, SEQ]) for u in range(2)]
        oout = [b.sb(f"a_oout{u}", [P, SEQ]) for u in range(2)]
        identb = b.sb("a_identb", [P, P], BF16)
        maskb = b.sb("a_maskb", [P, P], BF16)
        mx = [b.sb(f"a_mx{u}", [P, 2, HG, QT]) for u in range(2)]
        rest = b.sb("a_rest", [P, HG * QT])
        nm = b.sb("a_nm", [P, PARTS, HG * QT], BF16)
        nmt = b.sb("a_nmt", [PARTS * HG * QT, P], BF16)
        st_ps = [b.ps(f"a_st_ps{u}", [P, SEQ]) for u in range(2)]
        s_ps = [b.ps(f"a_s_ps{u}", [P, BANK]) for u in range(2)]
        o_ps = b.ps("a_o_ps", [P, SEQ])

        qk_loaded = [b.sem(f"a_qk_loaded{s}") for s in range(HG)]
        v_loaded = [b.sem(f"a_v_loaded{u}") for u in range(2)]
        ones_ready, consts, v_ready = b.sem("a_ones_ready"), b.sem("a_consts"), b.sem("a_v_ready")
        k_ones = b.sem("a_k_ones")
        piece_done, piece_maxed = b.sem("a_piece_done"), b.sem("a_piece_maxed")
        m_chain, nm_ready, nmt_done, nmt_ready, nm_stored = b.sem("a_m_chain"), b.sem("a_nm_ready"), b.sem("a_nmt_done"), b.sem("a_nmt_ready"), b.sem("a_nm_stored")
        st_done, exp_done, masked, av_done = b.sem("a_st_done"), b.sem("a_exp_done"), b.sem("a_masked"), b.sem("a_av_done")
        o_copied, pool_passed, sp_passed = b.sem("a_o_copied"), b.sem("a_pool_passed"), b.sem("a_sp_passed")
        o_stored = [b.sem(f"a_o_stored{u}") for u in range(2)]

        block = ctx.enter_context(nc.Block())

        def unit_ps(unit):
            kt, _, heads = UNITS[unit]
            width = SEQ - P * kt
            pitch = SEQ if heads == 1 else BANK if heads == 2 else width
            flat = st_ps[unit % 2][:] if heads == 1 else st_ps[unit % 2][:, 0:heads * pitch]
            if heads == 1:
                return flat[:, kt * P:SEQ].unsqueeze(1)
            return flat.rearrange("p (h n) -> p h n", n=pitch)[:, :, 0:width]

        def groups(eng, body):
            for hg in range(HG):
                body(0, hg, hg > 0, True)
            with eng.Fori(1, BATCH - 1) as bt:
                for hg in range(HG):
                    body(bt, hg, True, True)
            for hg in range(HG):
                body(BATCH - 1, hg, True, hg < HG - 1)

        @block.sync
        def _(sp):
            def load(bt, hg):
                seq = bass.ds(SEQ * bt, SEQ)
                for dst, src, order in ((qs, qd, (0, 0, 0, 1, 1, 2)), (ks, kd, (0, 1, 2, 0, 1, 0))):
                    for r, part in enumerate(order):
                        rows = src[HG * HD * hg:HG * HD * (hg + 1), part, seq].rearrange("(h d) n -> d h n", d=HD)
                        sp.dma_start(dst[hg][r * HD:(r + 1) * HD, :, :], rows).then_inc(qk_loaded[hg], 16)
                vr = vd[seq, HG * HD * hg:HG * HD * (hg + 1)].rearrange("(t p) d -> p t d", p=P)
                sp.dma_start(v_raw[hg % 2][:], vr).then_inc(v_loaded[hg % 2], 16)

            def store_max(n, slot):
                sp.wait_ge(nmt_ready, n + 2)
                for part in range(PARTS):
                    src = nmt[part * HG * QT:(part + 1) * HG * QT, :]
                    dst = qs[slot][STACK + part:STACK + part + 1, :, :].rearrange("a h (t q) -> a (h t) q", q=P)
                    sp.dma_start(dst, src).then_inc(nm_stored, 16)

            def store_o(n, bt, hg):
                wait_apart(sp, o_copied, n + 2, sp_passed)
                sp.dma_start(od[hg][:, bass.ds(SEQ * bt, SEQ)], oout[hg % 2][:]).then_inc(o_stored[hg % 2], 16)

            load(0, 0)
            load(0, 1)
            store_max(0, 0)

            def body(bt, hg, before, more):
                n = HG * bt + hg
                if hg < 2 or not (isinstance(bt, int) and bt == BATCH - 1):
                    if before:
                        wait_apart(sp, av_done, QT * n - 4, sp_passed)
                    wait_apart(sp, v_ready, n + 1, sp_passed)
                    load(bt + (hg + 2) // HG, (hg + 2) % HG)
                if before:
                    store_o(n - 1, *((bt, hg - 1) if hg else (bt - 1, HG - 1)))
                if more:
                    store_max(n + 1, (hg + 1) % HG)

            groups(sp, body)
            store_o(N_GROUPS - 1, BATCH - 1, HG - 1)
            for u in range(2):
                sp.wait_ge(o_stored[u], 16 * (N_GROUPS // 2 + 1))

        @block.gpsimd
        def _(pool):
            pool.sem_inc(masked, 1)
            nc.gpsimd.memset(identb[:], 0.0)
            nc.gpsimd.memset(maskb[:], 0.0)
            for u in range(2):
                i = nc.gpsimd.memset(va[u][:, :, :, HD:2 * HD], 1.0)
            i.then_inc(ones_ready, 1)
            pool.wait_ge(ones_ready, 1)
            nc.gpsimd.affine_select(out=identb[:], in_=identb[:], compare_op=ALU.not_equal, fill=1.0,
                                    base=0, pattern=[[-1, P]], channel_multiplier=1)
            nc.gpsimd.affine_select(out=maskb[:], in_=maskb[:], compare_op=ALU.is_ge, fill=NEG,
                                    base=0, pattern=[[-1, P]], channel_multiplier=1).then_inc(consts, 1)

            def augment(n, u, nth):
                wait_apart(pool, v_loaded[u], 16 * nth, pool_passed)
                nc.gpsimd.tensor_copy(va[u][:, :, :, 0:HD], v_raw[u][:].rearrange("p t (h d) -> p t h d", d=HD)).then_inc(v_ready, 1)

            augment(0, 0, 1)

            def body(bt, hg, before, more):
                n = HG * bt + hg
                for kt in range(QT):
                    wait_apart(pool, exp_done, NU * n + LAST_OF[kt] + 3, pool_passed)
                    diag = prob[kt % 2][:, :, kt * P:(kt + 1) * P]
                    nc.gpsimd.affine_select(out=diag, in_=diag, compare_op=ALU.is_ge, fill=0.0, base=0,
                                            pattern=[[0, HG], [1, P]], channel_multiplier=-1).then_inc(masked, 1)
                    if kt == 2 and more:
                        wait_apart(pool, av_done, QT * n + 2, pool_passed)
                        augment(n + 1, (hg + 1) % 2, 2 * bt + (hg + 1) // 2 + 1)

            groups(pool, body)

        @block.scalar
        def _(act):
            act.preload_act_table(ACT.Exp)
            act.sem_inc(exp_done, 2)
            act.sem_inc(o_copied, 1)
            for u in range(2):
                act.sem_inc(o_stored[u], 16)

            def body(bt, hg, before, more):
                n = HG * bt + hg
                for unit, (kt, j, heads) in enumerate(UNITS):
                    act.wait_ge(st_done, NU * n + unit + 1)
                    if unit == FIRST_OF[kt]:
                        act.wait_ge(av_done, QT * n + kt + 1)
                    nc.scalar.activation(prob[kt % 2][:, j:j + heads, kt * P:SEQ], unit_ps(unit), ACT.Exp).then_inc(exp_done, 1)
                    if unit == HG - 1 and before:
                        copy_o(n - 1, (hg + 1) % 2, 2 * bt + (hg + 1) // 2)

            def copy_o(n, u, nth):
                act.wait_ge(av_done, QT * n + QT + 2)
                act.wait_ge(o_stored[u], 16 * nth)
                nc.scalar.activation(oout[u][:], o_ps[:], ACT.Copy).then_inc(o_copied, 1)

            groups(act, body)
            copy_o(N_GROUPS - 1, 1, N_GROUPS // 2)

        @block.vector
        def _(dve):
            dve.sem_inc(piece_maxed, 2)
            for s in range(HG):
                i = nc.vector.memset(ks[s][STACK:ROWS, :, :], 1.0)
            i.then_inc(k_ones, 1)
            dve.sem_inc(nmt_ready, 1)
            CHAIN = 4

            def piece_max(n, p, u):
                j, qt, half = PIECES[p]
                width = min(P * (qt + 1) - BANK * half, BANK)
                dve.wait_ge(piece_done, NP * n + p + 1)
                nc.vector.reduce_max(mx[u][:, half, j, qt:qt + 1], s_ps[p % 2][:, 0:width], AX_X).then_inc(piece_maxed, 1)

            def negate(n, u):
                m = mx[u][:, 0, :, :].rearrange("p h t -> p (h t)")
                dve.wait_ge(piece_maxed, NP * (n + 1) + 2)
                nc.vector.tensor_tensor(mx[u][:, 0, :, QT // 2:QT], mx[u][:, 0, :, QT // 2:QT],
                                        mx[u][:, 1, :, QT // 2:QT], ALU.max).then_inc(m_chain, 1)
                dve.wait_ge(m_chain, CHAIN * n + 1)
                nc.vector.tensor_scalar(nm[:, 0, :], m, -1.0, None, ALU.mult).then_inc(m_chain, 1)
                dve.wait_ge(m_chain, CHAIN * n + 2)
                nc.vector.scalar_tensor_tensor(rest[:], m, -1.0, nm[:, 0, :], ALU.mult, ALU.subtract).then_inc(m_chain, 1)
                dve.wait_ge(m_chain, CHAIN * n + 3)
                nc.vector.tensor_copy(nm[:, 1, :], rest[:]).then_inc(m_chain, 1)
                dve.wait_ge(m_chain, CHAIN * n + 4)
                nc.vector.tensor_tensor(nm[:, 2, :], rest[:], nm[:, 1, :], ALU.subtract).then_inc(nm_ready, 1)
                dve.wait_ge(nmt_done, n + 1)
                dve.wait_ge(nm_stored, 16 * PARTS * n + 16)
                nc.vector.tensor_copy(nmt[:], s_ps[0][:].bitcast(BF16)[0:PARTS * HG * QT, 0:P]).then_inc(nmt_ready, 1)

            dve.sem_inc(nm_stored, 16)
            for p in range(NP):
                piece_max(0, p, 0)
            negate(0, 0)

            def body(bt, hg, before, more):
                if more:
                    n = HG * bt + hg + 1
                    for p in range(NP):
                        piece_max(n, p, (hg + 1) % 2)
                    negate(n, (hg + 1) % 2)

            groups(dve, body)

        @block.tensor
        def _(pe):
            pe.sem_inc(av_done, 2)

            def piece(n, p, slot):
                j, qt, half = PIECES[p]
                width = min(P * (qt + 1) - BANK * half, BANK)
                diagonal = qt // HG == half
                if p == 0:
                    pe.wait_ge(nmt_ready, n + 1)
                pe.wait_ge(piece_maxed, NP * n + p + 1)
                i = nc.tensor.matmul(s_ps[p % 2][:, 0:width], qs[slot][0:STACK, j, qt * P:(qt + 1) * P],
                                     ks[slot][0:STACK, j, half * BANK:half * BANK + width], start=True, stop=not diagonal)
                if diagonal:
                    i = nc.tensor.matmul(s_ps[p % 2][:, width - P:width], identb[:], maskb[:], start=False, stop=True)
                i.then_inc(piece_done, 1)

            def transpose_max(n):
                pe.wait_ge(nm_ready, n + 1)
                nc.tensor.transpose(s_ps[0][:].bitcast(BF16)[0:PARTS * HG * QT, 0:P], nm[:].rearrange("p a m -> p (a m)"),
                                    identb[:]).then_inc(nmt_done, 1)

            def segments(kt):
                return [(max(kt * P, lo), lo + BANK) for lo in range(0, SEQ, BANK) if kt * P < lo + BANK]

            def scores(n, unit, slot):
                kt, first, heads = UNITS[unit]
                if unit == 0:
                    pe.wait_ge(nm_stored, 16 * PARTS * (n + 1) + 16)
                pe.wait_ge(exp_done, NU * n + unit + 1)
                to = unit_ps(unit)
                for j in range(first, first + heads):
                    for lo, hi in segments(kt):
                        i = nc.tensor.matmul(to[:, j - first, lo - kt * P:hi - kt * P],
                                             ks[slot][0:ROWS, j, kt * P:(kt + 1) * P],
                                             qs[slot][0:ROWS, j, lo:hi], start=True, stop=True)
                i.then_inc(st_done, 1)

            def values(n, kt, u):
                pe.wait_ge(masked, QT * n + kt + 2)
                if kt == 0:
                    pe.wait_ge(v_ready, n + 1)
                    pe.wait_ge(o_copied, n + 1)
                for lo, hi in segments(kt):
                    for j in range(HG):
                        i = nc.tensor.matmul(o_ps[2 * HD * j:2 * HD * (j + 1), lo:hi], va[u][:, kt, j, :],
                                             prob[kt % 2][:, j, lo:hi], start=(kt == 0), stop=(kt * P + P == hi))
                i.then_inc(av_done, 1)

            pe.wait_ge(consts, 1)
            pe.wait_ge(k_ones, 1)
            pe.wait_ge(qk_loaded[0], 12 * 16)
            for p in range(NP):
                piece(0, p, 0)
            transpose_max(0)

            def body(bt, hg, before, more):
                n = HG * bt + hg
                nslot = (hg + 1) % HG
                p = 0
                transpose_at = None
                for unit, (kt, _, _) in enumerate(UNITS):
                    scores(n, unit, hg)
                    if more and unit == 0:
                        pe.wait_ge(qk_loaded[nslot], 12 * 16 * (bt + (hg + 1) // HG + 1))
                    if more:
                        for _ in range(AFTER[unit]):
                            piece(n + 1, p, nslot)
                            p += 1
                        if p == NP and transpose_at is None:
                            transpose_at = unit + 1
                        if unit == transpose_at:
                            transpose_max(n + 1)
                    if unit == 1 and before:
                        values(n - 1, QT - 1, (hg + 1) % 2)
                    if unit == LAST_OF[kt] and kt >= 1:
                        values(n, kt - 1, hg % 2)

            groups(pe, body)
            values(N_GROUPS - 1, QT - 1, 1)


def combine(nc, x, wout, out, scratch, keep):
    od, fd = scratch["o"], scratch["f"]
    ident = keep["ident"]
    N = TOK // P
    S = 8
    with ExitStack() as ctx:
        b = Bufs(nc, ctx)
        wo_raw = b.sb("c_wo_raw", [P, HALVES, DIM])
        woh = b.sb("c_woh", [P, HALVES, DIM], F32R)
        wol = b.sb("c_wol", [P, HALVES, DIM], F32R)
        ot = [b.sb(f"c_ot{s}", [P, HG, P]) for s in range(S)]
        f = [b.sb(f"c_f{s}", [P, DIM]) for s in range(S)]
        gate = [b.sb(f"c_gate{s}", [P, DIM]) for s in range(S)]
        xt = [b.sb(f"c_xt{s}", [P, DIM]) for s in range(S)]
        inv = [b.sb(f"c_inv{s}", [P, HEADS, 1]) for s in range(S)]
        on = [b.sb(f"c_on{s}", [P, HEADS, HD]) for s in range(S)]
        onh = [b.sb(f"c_onh{s}", [P, HALVES, P], F32R) for s in range(S)]
        onl = [b.sb(f"c_onl{s}", [P, HALVES, P], F32R) for s in range(S)]
        res = [b.sb(f"c_res{s}", [P, DIM]) for s in range(S)]
        t_ps = [b.ps(f"c_t_ps{u}", [P, HEADS, 2 * HD]) for u in range(2)]
        b_ps = [b.ps(f"c_b_ps{u}", [P, HALVES, P]) for u in range(2)]
        s_ps = [b.ps(f"c_s_ps{u}", [P, DIM]) for u in range(2)]

        w_loaded, w_high, w_split = b.sem("c_w_loaded"), b.sem("c_w_high"), b.sem("c_w_split")
        loaded = [b.sem(f"c_loaded{s}") for s in range(S)]
        heads_done, inv_done, divided, back_done = b.sem("c_heads_done"), b.sem("c_inv_done"), b.sem("c_divided"), b.sem("c_back_done")
        high_done, low_done, proj_done = b.sem("c_high_done"), b.sem("c_low_done"), b.sem("c_proj_done")
        gated, mixed, added = b.sem("c_gated"), b.sem("c_mixed"), b.sem("c_added")
        stored = [b.sem(f"c_stored{s}") for s in range(S)]

        block = ctx.enter_context(nc.Block())

        def steps(eng, lags, body):
            deepest = max(lags)

            def step(q, r):
                for k, lag in enumerate(lags):
                    i = S * q + r - lag
                    if isinstance(q, int) and not 0 <= i < N:
                        continue
                    body(k, i, (r - lag) % S, q + 1 + (r - lag) // S)

            assert deepest <= S
            for r in range(S):
                step(0, r)
            with eng.Fori(1, N // S) as q:
                for r in range(S):
                    step(q, r)
            for r in range(deepest):
                step(N // S, r)

        @block.sync
        def _(sp):
            sp.dma_start(wo_raw[:], wout.rearrange("(c p) n -> p c n", p=P)).then_inc(w_loaded, 16)

            def body(k, i, s, nth):
                tokens = bass.ds(P * i, P)
                if k == 0:
                    sp.wait_ge(added, i + 1)
                    sp.dma_start(ot[s][:], od[:, :, tokens].rearrange("h p n -> p h n")).then_inc(loaded[s], 16)
                    sp.dma_start(f[s][:], fd[tokens, :]).then_inc(loaded[s], 16)
                    sp.dma_start(xt[s][:], x[tokens, :]).then_inc(loaded[s], 16)
                else:
                    sp.wait_ge(added, i + S + 1)
                    sp.dma_start(out[tokens, :], res[s][:]).then_inc(stored[s], 16)

            steps(sp, (0, S - 1), body)
            for s in range(S):
                sp.wait_ge(stored[s], 16 * (N // S + 1))

        @block.gpsimd
        def _(pool):
            pool.sem_inc(added, S)

            def body(k, i, s, nth):
                pool.wait_ge(mixed, i + S + 1)
                nc.gpsimd.tensor_tensor(res[s][:], res[s][:], xt[s][:], ALU.add).then_inc(added, 1)

            steps(pool, (0,), body)

        @block.scalar
        def _(act):
            act.preload_act_table(ACT.Silu)
            for s in range(S):
                act.sem_inc(stored[s], 16)

            def body(k, i, s, nth):
                if k == 0:
                    act.wait_ge(loaded[s], 48 * nth)
                    act.wait_ge(mixed, i + 1)
                    nc.scalar.activation(gate[s][:], f[s][:], ACT.Silu).then_inc(gated, 1)
                else:
                    act.wait_ge(back_done, i + 1)
                    act.wait_ge(proj_done, i + 1)
                    nc.scalar.activation(onh[s][:], b_ps[s % 2][:], ACT.Copy).then_inc(high_done, 1)

            steps(act, (0, 1), body)

        @block.vector
        def _(dve):
            dve.sem_inc(divided, 2)
            dve.sem_inc(low_done, 2)
            dve.sem_inc(mixed, S)
            dve.wait_ge(w_loaded, 16)
            nc.vector.tensor_copy(woh[:], wo_raw[:]).then_inc(w_high, 1)
            dve.wait_ge(w_high, 1)
            nc.vector.tensor_tensor(wol[:], wo_raw[:], woh[:].bitcast(F32), ALU.subtract).then_inc(w_split, 1)

            def body(k, i, s, nth):
                if k == 0:
                    dve.wait_ge(heads_done, i + 1)
                    nc.vector.reciprocal(inv[s][:], t_ps[s % 2][:, :, HD:HD + 1]).then_inc(inv_done, 1)
                    dve.wait_ge(inv_done, i + 1)
                    nc.vector.tensor_tensor(on[s][:], t_ps[s % 2][:, :, 0:HD], inv[s][:].broadcast_to([P, HEADS, HD]),
                                            ALU.mult).then_inc(divided, 1)
                elif k == 1:
                    dve.wait_ge(high_done, i + 1)
                    nc.vector.tensor_tensor(onl[s][:], b_ps[s % 2][:], onh[s][:].bitcast(F32), ALU.subtract).then_inc(low_done, 1)
                else:
                    dve.wait_ge(proj_done, i + S + 1)
                    dve.wait_ge(gated, i + 1)
                    dve.wait_ge(stored[s], 16 * nth)
                    nc.vector.tensor_tensor(res[s][:], s_ps[s % 2][:], gate[s][:], ALU.mult).then_inc(mixed, 1)

            steps(dve, (0, 1, 2), body)

        @block.tensor
        def _(pe):
            pe.sem_inc(proj_done, S)
            pe.wait_ge(w_split, 1)

            def body(k, i, s, nth):
                u = s % 2
                if k == 0:
                    pe.wait_ge(loaded[s], 48 * nth)
                    pe.wait_ge(divided, i + 1)
                    for h in range(HG):
                        n = nc.tensor.transpose(t_ps[u][:, h * HG:(h + 1) * HG, :], ot[s][:, h, :], ident[:])
                    n.then_inc(heads_done, 1)
                elif k == 1:
                    pe.wait_ge(divided, i + 3)
                    pe.wait_ge(low_done, i + 1)
                    for c in range(HALVES):
                        n = nc.tensor.transpose(b_ps[u][:, c, :], on[s][:, c * P // HD:(c + 1) * P // HD, :].rearrange("p h d -> p (h d)"), ident[:])
                    n.then_inc(back_done, 1)
                else:
                    pe.wait_ge(low_done, i + 3)
                    pe.wait_ge(mixed, i + S - 1)
                    for c in range(HALVES):
                        for t, w in ((onh, woh), (onh, wol), (onl, woh)):
                            n = nc.tensor.matmul(s_ps[u][:], t[s][:, c, :], w[:, c, :],
                                                 start=(c == 0 and t is onh and w is woh), stop=(c == HALVES - 1 and t is onl))
                    n.then_inc(proj_done, 1)

            steps(pe, (0, 1, 2), body)


def gated_block(nc, x, wqkv, wout, w1t, b1, w2t, b2, ln_g, ln_b, out):
    scratch = {
        "q": nc.dram_tensor("q_parts", [DIM, PARTS, TOK], BF16, kind="Internal").ap(),
        "k": nc.dram_tensor("k_parts", [DIM, PARTS, TOK], BF16, kind="Internal").ap(),
        "v": nc.dram_tensor("values", [TOK, DIM], F32, kind="Internal").ap(),
        "f": nc.dram_tensor("mlp_out", [TOK, DIM], F32, kind="Internal").ap(),
        "o": nc.dram_tensor("attention_t", [HG, P, TOK], F32, kind="Internal").ap(),
    }
    with ExitStack() as ctx:
        b = Bufs(nc, ctx)
        keep = {"ident": b.sb("ident", [P, P]), "mhalf": b.sb("mhalf", [P, TILES])}
        with ExitStack() as inner:
            b = Bufs(nc, inner)
            keep |= {
                "xth": b.sb("xth", [P, HALVES, TOK], F32R),
                "xtl": b.sb("xtl", [P, HALVES, TOK], F32R),
                "xres": b.sb("xres", [P, TOK // P, DIM]),
                "y": [b.sb(f"y{u}", [P, TILES, DIM]) for u in range(2)],
            }
            project(nc, x, wqkv, scratch, keep)
            mlp(nc, w1t, w2t, b1, b2, ln_g, ln_b, scratch, keep)
        attend(nc, scratch)
        combine(nc, x, wout, out, scratch, keep)


def kernel(L0_attn_x, L0_attn_w_qkv, L0_attn_w_out, L0_ffn_W1, L0_ffn_B1, L0_ffn_W2, L0_ffn_B2, L0_ffn_LN_G, L0_ffn_LN_B):
    import numpy as np
    import concourse.bacc as bacc
    from concourse.bass_utils import run_bass_kernel_spmd

    nc = bacc.Bacc("TRN2", target_bir_lowering=False, num_devices=1)
    arrays = {
        "x": np.asarray(L0_attn_x).reshape(TOK, DIM),
        "w_qkv": np.asarray(L0_attn_w_qkv),
        "w_out": np.asarray(L0_attn_w_out),
        "w1t": np.asarray(L0_ffn_W1).transpose(0, 2, 1),
        "b1": np.asarray(L0_ffn_B1).reshape(BLOCKS, CH, P).transpose(0, 2, 1),
        "w2t": np.asarray(L0_ffn_W2).transpose(0, 2, 1),
        "b2": np.asarray(L0_ffn_B2),
        "ln_g": np.asarray(L0_ffn_LN_G),
        "ln_b": np.asarray(L0_ffn_LN_B),
    }
    arrays = {k: np.ascontiguousarray(v) for k, v in arrays.items()}
    args = [nc.dram_tensor(k, v.shape, mybir.dt.from_np(v.dtype), kind="ExternalInput").ap() for k, v in arrays.items()]
    out = nc.dram_tensor("out", [TOK, DIM], F32, kind="ExternalOutput").ap()
    gated_block(nc, *args, out)
    r = run_bass_kernel_spmd(nc, [arrays], core_ids=[0])
    return r.results[0]["out"].reshape(BATCH, SEQ, DIM)
```

```python
from contextlib import ExitStack

import concourse.bass as bass
from concourse import mybir

F32 = mybir.dt.float32
F32R = mybir.dt.float32r
BF16 = mybir.dt.bfloat16
ALU = mybir.AluOpType
ACT = mybir.ActivationFunctionType
AX_X = mybir.AxisListType.X

P = 128
BATCH, SEQ, DIM = 4, 1024, 256
TOK = BATCH * SEQ
HEADS, HD = 16, 16
HALVES = DIM // P
GT = 512
TILES = GT // P
GROUPS = TOK // GT
PAIRS = GROUPS // 2
BLOCKS = 6
HID = 4 * DIM
CH = HID // P
EPS = 1e-5
HG = 4
QT = SEQ // P
BANK = 512
PARTS = 3
STACK = 6 * HD
ROWS = STACK + PARTS
EARLY = 10
TURN = 6
DVE_COLUMN, DVE_START = 2.5, 150
ACT_COLUMN, ACT_START = 2.0, 500
TO_OTHER, TO_TENSOR = 600, 380
NEG = -1.0e30


class Bufs:

    def __init__(self, nc, ctx):
        self.nc, self.ctx = nc, ctx

    def sb(self, name, shape, dt=F32):
        return self.ctx.enter_context(self.nc.sbuf_tensor(name, shape, dt))

    def ps(self, name, shape, dt=F32):
        return self.ctx.enter_context(self.nc.psum_tensor(name, shape, dt))

    def sem(self, name):
        return self.ctx.enter_context(self.nc.semaphore(name))


def wait_apart(eng, sem, value, passed):
    eng.wait_ge(sem, value)
    eng.sem_inc(passed, 1)


def project(nc, x, wqkv, scratch, keep):
    qd, kd, vd = scratch["q"], scratch["k"], scratch["v"]
    xth, xtl, xres, y, ident = keep["xth"], keep["xtl"], keep["xres"], keep["y"], keep["ident"]
    with ExitStack() as ctx:
        b = Bufs(nc, ctx)
        xin = [b.sb(f"p_xin{u}", [P, TILES, DIM]) for u in range(2)]
        w_raw = b.sb("p_w_raw", [P, HALVES, 3 * DIM])
        wh = b.sb("p_wh", [P, HALVES, 3 * DIM], F32R)
        wl = b.sb("p_wl", [P, HALVES, 3 * DIM], F32R)
        gth = [b.sb(f"p_gth{u}", [P, HALVES, GT], F32R) for u in range(2)]
        gtl = [b.sb(f"p_gtl{u}", [P, HALVES, GT], F32R) for u in range(2)]
        part = [b.sb(f"p_part{m}", [P, PARTS, GT], BF16) for m in range(4)]
        rest = [b.sb(f"p_rest{m}", [P, GT]) for m in range(2)]
        vout = [b.sb(f"p_vout{u}", [P, TILES, DIM]) for u in range(2)]
        stats = [b.sb(f"p_stats{u}", [P, TILES, 6]) for u in range(2)]
        mv = [b.sb(f"p_mv{u}", [P, TILES, 2]) for u in range(2)]
        var = [b.sb(f"p_var{u}", [P, TILES]) for u in range(2)]
        rstd = [b.sb(f"p_rstd{u}", [P, TILES]) for u in range(2)]
        tr_ps = b.ps("p_tr_ps", [P, HALVES, GT])
        qk_ps = [b.ps(f"p_qk_ps{u}", [P, GT]) for u in range(2)]
        v_ps = b.ps("p_v_ps", [P, TILES, DIM])

        w_loaded, w_high, w_split = b.sem("p_w_loaded"), b.sem("p_w_high"), b.sem("p_w_split")
        x_loaded = [b.sem(f"p_x_loaded{u}") for u in range(2)]
        stats_done, mean_done, var_ready = b.sem("p_stats_done"), b.sem("p_mean_done"), b.sem("p_var_ready")
        rstd_ready, normed = b.sem("p_rstd_ready"), b.sem("p_normed")
        xres_stored = [b.sem(f"p_xres_stored{u}") for u in range(2)]
        gt_stored = [b.sem(f"p_gt_stored{u}") for u in range(2)]
        transposed, high_done, low_done = b.sem("p_transposed"), b.sem("p_high_done"), b.sem("p_low_done")
        qk_done, part0_done, rest_done = b.sem("p_qk_done"), b.sem("p_part0_done"), b.sem("p_rest_done")
        part1_done, part2_done = b.sem("p_part1_done"), b.sem("p_part2_done")
        part_stored = [b.sem(f"p_part_stored{m}") for m in range(4)]
        v_done, v_copied = b.sem("p_v_done"), b.sem("p_v_copied")
        v_stored = [b.sem(f"p_v_stored{u}") for u in range(2)]
        ident_ready = b.sem("p_ident_ready")
        half_ready, passed = b.sem("p_half_ready"), b.sem("p_passed")

        block = ctx.enter_context(nc.Block())

        def pairs(eng, body):
            with eng.Fori(0, PAIRS - 1) as p:
                body(p, False)
            body(PAIRS - 1, True)

        @block.sync
        def _(sp):
            sp.dma_start(w_raw[:], wqkv.rearrange("(c p) n -> p c n", p=P)).then_inc(w_loaded, 16)
            xg = x.rearrange("(g j p) d -> g p j d", p=P, j=TILES)

            def load_x(g, u):
                sp.dma_start(xin[u][:], xg[g]).then_inc(x_loaded[u], 16)

            load_x(0, 0)
            load_x(1, 1)

            def body(p, last):
                for u in range(2):
                    g = 2 * p + u
                    sp.wait_ge(normed, g + 3)
                    sp.dma_start(xres[:, bass.ds(TILES * g, TILES), :], y[u][:]).then_inc(xres_stored[u], 16)
                    if not last:
                        load_x(g + 2, u)
                    sp.wait_ge(low_done, g + 2)
                    sp.dma_start(xth[:, :, bass.ds(GT * g, GT)].bitcast(F32), gth[u][:].bitcast(F32)).then_inc(gt_stored[u], 16)
                    sp.dma_start(xtl[:, :, bass.ds(GT * g, GT)].bitcast(F32), gtl[u][:].bitcast(F32)).then_inc(gt_stored[u], 16)

            pairs(sp, body)
            for u in range(2):
                sp.wait_ge(xres_stored[u], 16 * (PAIRS + 1))
                sp.wait_ge(gt_stored[u], 32 * (PAIRS + 1))

        @block.gpsimd
        def _(pool):
            nc.gpsimd.memset(ident[:], 0.0).then_inc(ident_ready, 1)
            nc.gpsimd.memset(keep["mhalf"][:], -0.5).then_inc(half_ready, 1)
            pool.wait_ge(ident_ready, 1)
            nc.gpsimd.affine_select(out=ident[:], in_=ident[:], compare_op=ALU.not_equal, fill=1.0,
                                    base=0, pattern=[[-1, P]], channel_multiplier=1).then_inc(ident_ready, 1)
            pool.wait_ge(half_ready, 1)

            with pool.Fori(0, PAIRS) as p:
                for u in range(2):
                    pool.wait_ge(var_ready, 2 * p + u + 1)
                    nc.gpsimd.tensor_tensor(rstd[u][:], var[u][:], keep["mhalf"][:], ALU.pow).then_inc(rstd_ready, 1)

        @block.vector
        def _(dve):
            dve.sem_inc(normed, 2)
            dve.sem_inc(low_done, 1)
            dve.sem_inc(rest_done, 2)
            dve.sem_inc(part2_done, 2)
            dve.wait_ge(w_loaded, 16)
            nc.vector.tensor_copy(wh[:], w_raw[:]).then_inc(w_high, 1)
            dve.wait_ge(w_high, 1)
            nc.vector.tensor_tensor(wl[:], w_raw[:], wh[:].bitcast(F32), ALU.subtract).then_inc(w_split, 1)

            def norm(g, u, n):
                dve.wait_ge(x_loaded[u], 16 * n)
                for j in range(TILES):
                    i = nc.vector.bn_stats(stats[u][:, j, :], xin[u][:, j, :])
                i.then_inc(stats_done, 1)
                wait_apart(dve, stats_done, g + 1, passed)
                for j in range(TILES):
                    i = nc.vector.bn_aggr(mv[u][:, j, :], stats[u][:, j, :])
                i.then_inc(mean_done, 1)
                dve.wait_ge(mean_done, g + 1)
                nc.vector.tensor_scalar(var[u][:], mv[u][:, :, 1], EPS, None, ALU.add).then_inc(var_ready, 1)
                dve.wait_ge(transposed, g + 1)
                dve.wait_ge(xres_stored[u], 16 * n)
                dve.wait_ge(rstd_ready, g + 1)
                for j in range(TILES):
                    i = nc.vector.tensor_scalar(y[u][:, j, :], xin[u][:, j, :], mv[u][:, j, 0:1],
                                                rstd[u][:, j:j + 1], ALU.subtract, ALU.mult)
                i.then_inc(normed, 1)

            def low(g, u):
                dve.wait_ge(high_done, g + 1)
                nc.vector.tensor_tensor(gtl[u][:], tr_ps[:], gth[u][:].bitcast(F32), ALU.subtract).then_inc(low_done, 1)

            def split_rest(g, m):
                dve.wait_ge(part0_done, 4 * g + m + 1)
                dve.wait_ge(part2_done, 4 * g + m + 1)
                nc.vector.scalar_tensor_tensor(rest[m % 2][:], qk_ps[m % 2][:], 0.25 if m < 2 else 1.0,
                                               part[m][:, 0, :], ALU.mult, ALU.subtract).then_inc(rest_done, 1)

            def split_last(g, m):
                dve.wait_ge(part1_done, 4 * g + m + 1)
                nc.vector.tensor_tensor(part[m][:, 2, :], rest[m % 2][:], part[m][:, 1, :],
                                        ALU.subtract).then_inc(part2_done, 1)

            norm(0, 0, 1)
            low(0, 0)

            def body(p, last):
                for u in range(2):
                    g = 2 * p + u
                    more = not (last and u == 1)
                    if more:
                        norm(g + 1, 1 - u, p + 1 + u)
                    split_rest(g, 0)
                    split_rest(g, 1)
                    split_last(g, 0)
                    split_last(g, 1)
                    split_rest(g, 2)
                    split_rest(g, 3)
                    split_last(g, 2)
                    if more:
                        low(g + 1, 1 - u)
                    split_last(g, 3)

            pairs(dve, body)

        @block.scalar
        def _(act):
            act.sem_inc(v_copied, 1)
            for u in range(2):
                act.sem_inc(xres_stored[u], 16)
                act.sem_inc(gt_stored[u], 32)
                act.sem_inc(v_stored[u], 16)
            for m in range(4):
                act.sem_inc(part_stored[m], 16)

            def high(g, u, n):
                act.wait_ge(transposed, g + 3)
                act.wait_ge(v_done, g + 1)
                act.wait_ge(gt_stored[u], 32 * n)
                nc.scalar.activation(gth[u][:], tr_ps[:], ACT.Copy).then_inc(high_done, 1)

            def part0(g, m):
                act.wait_ge(qk_done, 4 * g + m + 1)
                act.wait_ge(part_stored[m], 16 * g + 16)
                nc.scalar.activation(part[m][:, 0, :], qk_ps[m % 2][:], ACT.Copy,
                                     scale=0.25 if m < 2 else 1.0).then_inc(part0_done, 1)

            def part1(g, m):
                act.wait_ge(rest_done, 4 * g + m + 3)
                nc.scalar.activation(part[m][:, 1, :], rest[m % 2][:], ACT.Copy).then_inc(part1_done, 1)

            def store(g, m):
                act.wait_ge(part2_done, 4 * g + m + 3)
                rows = (qd if m < 2 else kd)[P * (m % 2):P * (m % 2) + P]
                act.dma_start(rows[:, :, bass.ds(GT * g, GT)], part[m][:]).then_inc(part_stored[m], 16)

            high(0, 0, 1)

            def body(p, last):
                for u in range(2):
                    g = 2 * p + u
                    part0(g, 0)
                    part0(g, 1)
                    part1(g, 0)
                    part1(g, 1)
                    part0(g, 2)
                    part0(g, 3)
                    part1(g, 2)
                    store(g, 0)
                    if not (last and u == 1):
                        high(g + 1, 1 - u, p + 1 + u)
                    part1(g, 3)
                    store(g, 1)
                    store(g, 2)
                    act.wait_ge(v_done, g + 3)
                    act.wait_ge(v_stored[u], 16 * p + 16)
                    nc.scalar.activation(vout[u][:], v_ps[:], ACT.Copy).then_inc(v_copied, 1)
                    store(g, 3)
                    act.wait_ge(v_copied, g + 2)
                    act.dma_start(vd.rearrange("(g j p) d -> g p j d", p=P, j=TILES)[g], vout[u][:]).then_inc(v_stored[u], 16)

            pairs(act, body)
            for m in range(4):
                act.wait_ge(part_stored[m], 16 * (GROUPS + 1))
            for u in range(2):
                act.wait_ge(v_stored[u], 16 * (PAIRS + 1))

        @block.tensor
        def _(pe):
            pe.sem_inc(transposed, 2)
            pe.sem_inc(v_done, 2)
            pe.wait_ge(ident_ready, 2)

            def transpose(g, u):
                pe.wait_ge(normed, g + 3)
                pe.wait_ge(low_done, g + 1)
                for c in range(HALVES):
                    for j in range(TILES):
                        i = nc.tensor.transpose(tr_ps[:, c, j * P:(j + 1) * P], y[u][:, j, c * P:(c + 1) * P], ident[:])
                i.then_inc(transposed, 1)

            transpose(0, 0)
            pe.wait_ge(w_split, 1)

            def body(p, last):
                for u in range(2):
                    g = 2 * p + u
                    pe.wait_ge(low_done, g + 2)
                    for m in range(4):
                        pe.wait_ge(rest_done, 4 * g + m + 1)
                        cols = slice(P * m, P * m + P)
                        for c in range(HALVES):
                            for w, t in ((wh, gth), (wh, gtl), (wl, gth)):
                                i = nc.tensor.matmul(qk_ps[m % 2][:], w[:, c, cols], t[u][:, c, :],
                                                     start=(c == 0 and w is wh and t is gth),
                                                     stop=(c == HALVES - 1 and w is wl))
                        i.then_inc(qk_done, 1)
                    if not (last and u == 1):
                        transpose(g + 1, 1 - u)
                    pe.wait_ge(v_copied, g + 1)
                    for j in range(TILES):
                        for c in range(HALVES):
                            for t, w in ((gth, wh), (gth, wl), (gtl, wh)):
                                first = c == 0 and t is gth and w is wh
                                i = nc.tensor.matmul(v_ps[:, j, :], t[u][:, c, j * P:(j + 1) * P],
                                                     w[:, c, 2 * DIM:3 * DIM], start=(first and j % 2 == 0),
                                                     stop=(c == HALVES - 1 and t is gtl), skip_group_check=True)
                    i.then_inc(v_done, 1)

            pairs(pe, body)


def mlp(nc, w1t, w2t, b1, b2, ln_g, ln_b, scratch, keep):
    fd = scratch["f"]
    xth, xtl, xres, y, ident = keep["xth"], keep["xtl"], keep["xres"], keep["y"], keep["ident"]
    SLOTS = BLOCKS * GROUPS
    with ExitStack() as ctx:
        b = Bufs(nc, ctx)
        raw1 = [b.sb(f"m_raw1{u}", [P, HALVES, P]) for u in range(2)]
        raw2 = [b.sb(f"m_raw2{u}", [P, DIM]) for u in range(2)]
        w1h = [b.sb(f"m_w1h{u}", [P, HALVES, HID], F32R) for u in range(2)]
        w1l = [b.sb(f"m_w1l{u}", [P, HALVES, HID], F32R) for u in range(2)]
        w2h = [b.sb(f"m_w2h{u}", [P, CH, DIM], F32R) for u in range(2)]
        w2l = [b.sb(f"m_w2l{u}", [P, CH, DIM], F32R) for u in range(2)]
        b1s = [b.sb(f"m_b1s{u}", [P, CH]) for u in range(2)]
        b2s = [b.sb(f"m_b2s{u}", [P, 1, DIM]) for u in range(2)]
        lng = [b.sb(f"m_lng{u}", [P, DIM]) for u in range(2)]
        lnb = [b.sb(f"m_lnb{u}", [P, DIM]) for u in range(2)]
        hid = [b.sb(f"m_hid{k}", [P, GT]) for k in range(2)]
        hidh = [b.sb(f"m_hidh{k}", [P, GT], F32R) for k in range(4)]
        hidl = [b.sb(f"m_hidl{k}", [P, GT], F32R) for k in range(4)]
        stats = b.sb("m_stats", [P, TILES, 6])
        mv = b.sb("m_mv", [P, TILES, 2])
        var = b.sb("m_var", [P, TILES])
        rstd = b.sb("m_rstd", [P, TILES])
        h_ps = [b.ps(f"m_h_ps{k}", [P, GT]) for k in range(2)]
        y_ps = [b.ps(f"m_y_ps{u}", [P, TILES, DIM]) for u in range(2)]
        tr_ps = b.ps("m_tr_ps", [P, HALVES, GT])

        raw_loaded = [b.sem(f"m_raw_loaded{u}") for u in range(2)]
        bias_loaded = [b.sem(f"m_bias_loaded{u}") for u in range(2)]
        ln_loaded = [b.sem(f"m_ln_loaded{u}") for u in range(2)]
        w_high, w_split = b.sem("m_w_high"), b.sem("m_w_split")
        w1_done, gelu_done, low_done = b.sem("m_w1_done"), b.sem("m_gelu_done"), b.sem("m_low_done")
        w2_done, y_added, b2_added = b.sem("m_w2_done"), b.sem("m_y_added"), b.sem("m_b2_added")
        stats_done, mean_done, var_ready = b.sem("m_stats_done"), b.sem("m_mean_done"), b.sem("m_var_ready")
        rstd_ready, scaled, x_ready = b.sem("m_rstd_ready"), b.sem("m_scaled"), b.sem("m_x_ready")
        transposed, xth_done, xtl_done = b.sem("m_transposed"), b.sem("m_xth_done"), b.sem("m_xtl_done")
        xres_done, passed = b.sem("m_xres_done"), b.sem("m_passed")
        f_stored = [b.sem(f"m_f_stored{u}") for u in range(2)]

        block = ctx.enter_context(nc.Block())

        class Slot:

            def __init__(s, i, gp, u, par, nth, kind, first):
                s.i, s.gp, s.u, s.par, s.nth, s.kind = i, gp, u, par, nth, kind
                s.g = 2 * gp + u
                s.t = GROUPS * i + s.g
                s.seam = first and u == 0
                s.start = kind == "first" and s.seam
                s.second = kind == "first" and first and u == 1
                s.epar = 1 - par if s.seam else par
                s.enth = nth - (1 - par) if s.seam else nth
                s.eg = GROUPS - 1 if s.seam else s.g - 1
                s.first = first
                s.final = kind == "last" and not s.seam
                s.more = kind != "last"

        def sweep(eng, slot, begin=None):
            def one(i, par, nth, kind):
                if begin:
                    begin(i, par, nth, kind)
                for u in range(2):
                    slot(Slot(i, 0, u, par, nth, kind, True))
                with eng.Fori(1, PAIRS) as gp:
                    for u in range(2):
                        slot(Slot(i, gp, u, par, nth, kind, False))

            one(0, 0, 1, "first")
            with eng.Fori(0, (BLOCKS - 2) // 2) as q:
                one(2 * q + 1, 1, q + 1, "middle")
                one(2 * q + 2, 0, q + 2, "middle")
            one(BLOCKS - 1, 1, BLOCKS // 2, "last")

        @block.sync
        def _(sp):
            w1v = w1t.rearrange("i (c p) h -> i p c h", p=P)

            def load_raw(i, g, u):
                sp.dma_start(raw1[u][:], w1v[i][:, :, bass.ds(P * g, P)]).then_inc(raw_loaded[u], 16)
                sp.dma_start(raw2[u][:], w2t[i, bass.ds(P * g, P), :]).then_inc(raw_loaded[u], 16)

            def load_bias(i, par):
                sp.dma_start(b1s[par][:], b1[i]).then_inc(bias_loaded[par], 16)
                sp.dma_start(b2s[par][:, 0, :], b2[bass.ds(i, 1), :].broadcast_to([P, DIM])).then_inc(bias_loaded[par], 16)

            for g in range(GROUPS):
                if g >= 2:
                    sp.wait_ge(w_split, g - 1)
                load_raw(0, g, g % 2)
                if g == 0:
                    load_bias(0, 0)

            def begin(i, par, nth, kind):
                if kind == "last":
                    return
                if kind == "middle":
                    sp.wait_ge(x_ready, GROUPS * i - 7)
                sp.dma_start(lng[par][:], ln_g[bass.ds(i, 1), :].broadcast_to([P, DIM])).then_inc(ln_loaded[par], 16)
                sp.dma_start(lnb[par][:], ln_b[bass.ds(i, 1), :].broadcast_to([P, DIM])).then_inc(ln_loaded[par], 16)

            def slot(s):
                if s.more:
                    piece = GROUPS * (s.i + 1) + s.g
                    sp.wait_ge(w_split, piece - 1)
                    load_raw(s.i + 1, s.g, s.u)
                    if s.second or (s.kind == "middle" and s.first and s.u == 1):
                        if s.kind == "middle":
                            sp.wait_ge(b2_added, GROUPS * s.i)
                        load_bias(s.i + 1, 1 - s.par)
                if s.final:
                    store_f(s.t, s.eg, s.epar, (s.u + 1) % 2)

            def store_f(t, eg, epar, yu):
                sp.wait_ge(b2_added, t)
                sp.dma_start(fd.rearrange("(g j p) d -> g p j d", p=P, j=TILES)[eg], y[yu][:]).then_inc(f_stored[yu], 16)

            sweep(sp, slot, begin)
            store_f(SLOTS, GROUPS - 1, 1, 1)
            for u in range(2):
                sp.wait_ge(f_stored[u], 16 * (PAIRS + 1))

        @block.gpsimd
        def _(pool):
            def slot(s):
                if not s.start:
                    add_b2(s.t, s.epar, 1 - s.u)
                    if not s.final:
                        pool.wait_ge(var_ready, s.t)
                        nc.gpsimd.tensor_tensor(rstd[:], var[:], keep["mhalf"][:], ALU.pow).then_inc(rstd_ready, 1)

            def add_b2(t, epar, yu):
                pool.wait_ge(y_added, t + 2)
                nc.gpsimd.tensor_tensor(y[yu][:], y[yu][:], b2s[epar][:].broadcast_to([P, TILES, DIM]),
                                        ALU.add).then_inc(b2_added, 1)

            def begin(i, par, nth, kind):
                pool.wait_ge(bias_loaded[par], 32 * nth)

            sweep(pool, slot, begin)
            add_b2(SLOTS, 1, 1)

        @block.scalar
        def _(act):
            act.preload_act_table(ACT.Gelu)
            act.sem_inc(gelu_done, 2)
            act.sem_inc(xres_done, 1)
            for u in range(2):
                act.sem_inc(f_stored[u], 16)

            def begin(i, par, nth, kind):
                act.wait_ge(bias_loaded[par], 32 * nth)

            def slot(s):
                for k in range(CH):
                    n = CH * s.t + k
                    act.wait_ge(w1_done, n + 1)
                    act.wait_ge(low_done, n + 1)
                    nc.scalar.activation(hid[k % 2][:], h_ps[k % 2][:], ACT.Gelu, bias=b1s[s.par][:, k:k + 1])
                    act.wait_ge(w2_done, n + 1)
                    nc.scalar.activation(hidh[k % 4][:], h_ps[k % 2][:], ACT.Gelu, bias=b1s[s.par][:, k:k + 1]).then_inc(gelu_done, 1)
                if s.start or s.final:
                    return
                act.wait_ge(transposed, s.t + 1)
                nc.scalar.activation(xth[:, :, bass.ds(GT * s.eg, GT)], tr_ps[:], ACT.Copy).then_inc(xth_done, 1)
                act.wait_ge(x_ready, s.t + 1)
                nc.scalar.activation(xres[:, bass.ds(TILES * s.eg, TILES), :], y[1 - s.u][:], ACT.Copy).then_inc(xres_done, 1)

            sweep(act, slot, begin)

        @block.vector
        def _(dve):
            dve.sem_inc(low_done, 2)
            dve.sem_inc(y_added, 2)
            dve.sem_inc(x_ready, 1)

            def split_weights(i, g, u, par, nth):
                piece = GROUPS * i + g
                cols = bass.ds(P * g, P)
                dve.wait_ge(raw_loaded[u], 32 * nth)
                nc.vector.tensor_copy(w1h[par][:, :, cols], raw1[u][:])
                nc.vector.tensor_copy(w2h[par][:, bass.ds(g, 1), :].squeeze(1), raw2[u][:]).then_inc(w_high, 1)
                dve.wait_ge(w_high, piece + 1)
                nc.vector.tensor_tensor(w1l[par][:, :, cols], raw1[u][:], w1h[par][:, :, cols].bitcast(F32), ALU.subtract)
                nc.vector.tensor_tensor(w2l[par][:, bass.ds(g, 1), :].squeeze(1), raw2[u][:], w2h[par][:, bass.ds(g, 1), :].squeeze(1).bitcast(F32),
                                        ALU.subtract).then_inc(w_split, 1)

            for g in range(GROUPS):
                split_weights(0, g, g % 2, 0, g // 2 + 1)

            def add_y(t, eg, yu):
                dve.wait_ge(w2_done, CH * t + 4)
                nc.vector.tensor_tensor(y[yu][:], y_ps[yu][:], xres[:, bass.ds(TILES * eg, TILES), :],
                                        ALU.add).then_inc(y_added, 1)

            def slot(s):
                epilogue = not (s.start or s.final)
                if not s.start:
                    if s.kind == "last" and not s.first:
                        dve.wait_ge(f_stored[1 - s.u], 16 * s.gp + 16 * s.u)
                        dve.wait_ge(transposed, GROUPS * (BLOCKS - 1) + 1)
                        dve.wait_ge(xres_done, GROUPS * (BLOCKS - 1) + 1)
                    elif not s.second:
                        dve.wait_ge(transposed, s.t - 1)
                        dve.wait_ge(xres_done, s.t - 1)
                    add_y(s.t, s.eg, 1 - s.u)
                yy = y[1 - s.u]
                for k in range(CH):
                    n = CH * s.t + k
                    dve.wait_ge(gelu_done, n + 3)
                    nc.vector.tensor_tensor(hidl[k % 4][:], hid[k % 2][:], hidh[k % 4][:].bitcast(F32),
                                            ALU.subtract).then_inc(low_done, 1)
                    if k == 1 and epilogue:
                        dve.wait_ge(b2_added, s.t)
                        for j in range(TILES):
                            i = nc.vector.bn_stats(stats[:, j, :], yy[:, j, :])
                        i.then_inc(stats_done, 1)
                    if k == 2 and epilogue:
                        wait_apart(dve, stats_done, s.t, passed)
                        for j in range(TILES):
                            i = nc.vector.bn_aggr(mv[:, j, :], stats[:, j, :])
                        i.then_inc(mean_done, 1)
                    if k == 3 and epilogue:
                        dve.wait_ge(mean_done, s.t)
                        nc.vector.tensor_scalar(var[:], mv[:, :, 1], EPS, None, ALU.add).then_inc(var_ready, 1)
                        dve.wait_ge(ln_loaded[s.epar], 32 * s.enth)
                        for j in range(TILES):
                            i = nc.vector.scalar_tensor_tensor(yy[:, j, :], yy[:, j, :], mv[:, j, 0:1], lng[s.epar][:],
                                                               ALU.subtract, ALU.mult)
                        i.then_inc(scaled, 1)
                    if k == 4 and s.more:
                        split_weights(s.i + 1, s.g, s.u, 1 - s.par, 4 * (s.i + 1) + s.gp + 1)
                    if k == 5 and epilogue:
                        dve.wait_ge(scaled, s.t)
                        dve.wait_ge(rstd_ready, s.t)
                        for j in range(TILES):
                            i = nc.vector.scalar_tensor_tensor(yy[:, j, :], yy[:, j, :], rstd[:, j:j + 1], lnb[s.epar][:],
                                                               ALU.mult, ALU.add)
                        i.then_inc(x_ready, 1)
                if epilogue:
                    cols = bass.ds(GT * s.eg, GT)
                    dve.wait_ge(xth_done, s.t)
                    nc.vector.tensor_tensor(xtl[:, :, cols], tr_ps[:], xth[:, :, cols].bitcast(F32),
                                            ALU.subtract).then_inc(xtl_done, 1)

            sweep(dve, slot)
            dve.wait_ge(f_stored[1], 16 * PAIRS)
            add_y(SLOTS, GROUPS - 1, 1)

        @block.tensor
        def _(pe):
            pe.sem_inc(w2_done, 4)
            pe.sem_inc(transposed, 1)

            def begin(i, par, nth, kind):
                pe.wait_ge(w_split, GROUPS * (i + 1))

            def slot(s):
                tokens = bass.ds(GT * s.g, GT)

                def up(k):
                    pe.wait_ge(gelu_done, CH * s.t + k + 1)
                    for c in range(HALVES):
                        for w, x in ((w1h, xth), (w1h, xtl), (w1l, xth)):
                            i = nc.tensor.matmul(h_ps[k % 2][:], w[s.par][:, c, k * P:(k + 1) * P], x[:, c, tokens],
                                                 start=(c == 0 and w is w1h and x is xth), stop=(c == HALVES - 1 and w is w1l))
                    i.then_inc(w1_done, 1)

                def down(k):
                    pe.wait_ge(low_done, CH * s.t + k + 3)
                    if k == 0:
                        pe.wait_ge(y_added, s.t + 1)
                    for j in range(TILES):
                        for h, w in ((hidh, w2h), (hidh, w2l), (hidl, w2h)):
                            i = nc.tensor.matmul(y_ps[s.u][:, j, :], h[k % 4][:, j * P:(j + 1) * P], w[s.par][:, k, :],
                                                 start=(k == 0 and j % 2 == 0 and h is hidh and w is w2h),
                                                 stop=(k == CH - 1 and h is hidl), skip_group_check=True)
                    i.then_inc(w2_done, 1)

                if s.kind != "first":
                    pe.wait_ge(xtl_done, s.t - 7)
                for k in range(CH):
                    up(k)
                    if k >= 2:
                        down(k - 2)
                if not (s.start or s.final):
                    pe.wait_ge(x_ready, s.t + 1)
                    if not s.second:
                        pe.wait_ge(xtl_done, s.t - 1)
                    for c in range(HALVES):
                        for j in range(TILES):
                            i = nc.tensor.transpose(tr_ps[:, c, j * P:(j + 1) * P],
                                                    y[1 - s.u][:, j, c * P:(c + 1) * P], ident[:])
                    i.then_inc(transposed, 1)
                down(CH - 2)
                down(CH - 1)

            sweep(pe, slot, begin)


def max_pieces():
    pieces = []
    for qt in range(QT):
        for half in range(1 + qt // HG):
            keys = min(P * (qt + 1) - BANK * half, BANK)
            heads = min(BANK // keys, HG)
            pieces += [(qt, half, j, heads, keys) for j in range(0, HG, heads)]
    return pieces


def score_units():
    per = {kt: 1 if kt < 4 else 2 if kt < 6 else HG for kt in range(QT)}
    return [(kt, j, per[kt]) for kt in range(QT) for j in range(0, HG, per[kt])]


def segments(kt):
    return [(max(kt * P, lo), lo + BANK) for lo in range(0, SEQ, BANK) if kt * P < lo + BANK]


def attend(nc, scratch):
    qd, kd, vd, od = scratch["q"], scratch["k"], scratch["v"], scratch["o"]
    N_GROUPS = BATCH * HG
    PIECES = max_pieces()
    NP = len(PIECES)
    UNITS = score_units()
    NU = len(UNITS)
    CHAIN = 5
    LAST_OF = {kt: max(n for n, unit in enumerate(UNITS) if unit[0] == kt) for kt in range(QT)}
    FIRST_OF = {kt: min(n for n, unit in enumerate(UNITS) if unit[0] == kt) for kt in range(QT)}
    with ExitStack() as ctx:
        b = Bufs(nc, ctx)
        qs = [b.sb(f"a_qs{s}", [P, HG, SEQ], BF16) for s in range(HG)]
        ks = [b.sb(f"a_ks{s}", [P, HG, SEQ], BF16) for s in range(HG)]
        v_raw = [b.sb(f"a_v_raw{u}", [P, QT, HG * HD]) for u in range(2)]
        va = [b.sb(f"a_va{u}", [P, QT, HG, 2 * HD]) for u in range(2)]
        prob = [b.sb(f"a_prob{u}", [P, HG, SEQ]) for u in range(2)]
        oout = [b.sb(f"a_oout{u}", [P, SEQ]) for u in range(2)]
        identb = b.sb("a_identb", [P, P], BF16)
        maskb = b.sb("a_maskb", [P, P], BF16)
        mx = [b.sb(f"a_mx{u}", [P, 2, HG, QT]) for u in range(2)]
        rest = b.sb("a_rest", [P, HG * QT])
        nm = b.sb("a_nm", [P, PARTS, HG * QT], BF16)
        nmt = b.sb("a_nmt", [PARTS * HG * QT, P], BF16)
        st_ps = [b.ps(f"a_st_ps{u}", [P, SEQ]) for u in range(2)]
        s_ps = [b.ps(f"a_s_ps{u}", [P, BANK]) for u in range(2)]
        o_ps = b.ps("a_o_ps", [P, SEQ])

        qk_loaded = [b.sem(f"a_qk_loaded{s}") for s in range(HG)]
        v_loaded = [b.sem(f"a_v_loaded{u}") for u in range(2)]
        cleared, consts, v_ready = b.sem("a_cleared"), b.sem("a_consts"), b.sem("a_v_ready")
        k_ones = b.sem("a_k_ones")
        piece_done, piece_maxed = b.sem("a_piece_done"), b.sem("a_piece_maxed")
        m_chain, nm_ready, nmt_done, nmt_ready, nm_stored = b.sem("a_m_chain"), b.sem("a_nm_ready"), b.sem("a_nmt_done"), b.sem("a_nmt_ready"), b.sem("a_nm_stored")
        st_done, exp_done, masked, av_done = b.sem("a_st_done"), b.sem("a_exp_done"), b.sem("a_masked"), b.sem("a_av_done")
        o_copied, pool_passed, sp_passed = b.sem("a_o_copied"), b.sem("a_pool_passed"), b.sem("a_sp_passed")
        o_stored = [b.sem(f"a_o_stored{u}") for u in range(2)]

        block = ctx.enter_context(nc.Block())

        def unit_ps(unit):
            kt, _, heads = UNITS[unit]
            width = SEQ - P * kt
            pitch = SEQ if heads == 1 else BANK if heads == 2 else width
            flat = st_ps[unit % 2][:] if heads == 1 else st_ps[unit % 2][:, 0:heads * pitch]
            if heads == 1:
                return flat[:, kt * P:SEQ].unsqueeze(1)
            return flat.rearrange("p (h n) -> p h n", n=pitch)[:, :, 0:width]

        def search_bank(hg, p):
            return (hg + p + (p >= TURN)) % 2

        def piece_ps(hg, p):
            _, _, _, heads, keys = PIECES[p]
            return s_ps[search_bank(hg, p)][:, 0:heads * keys].rearrange("p (h n) -> p h n", n=keys)

        def turned(hg):
            return s_ps[(hg + 1 + TURN) % 2][:].bitcast(BF16)[0:PARTS * HG * QT, 0:P]

        def groups(eng, body):
            for hg in range(HG):
                body(0, hg, hg > 0, 2)
            with eng.Fori(1, BATCH - 1) as bt:
                for hg in range(HG):
                    body(bt, hg, True, 2)
            for hg in range(HG):
                body(BATCH - 1, hg, True, min(2, HG - 1 - hg))

        @block.sync
        def _(sp):
            def load(bt, hg):
                seq = bass.ds(SEQ * bt, SEQ)
                for dst, src, order in ((qs, qd, (0, 0, 0, 1, 1, 2)), (ks, kd, (0, 1, 2, 0, 1, 0))):
                    for r, part in enumerate(order):
                        rows = src[HG * HD * hg:HG * HD * (hg + 1), part, seq].rearrange("(h d) n -> d h n", d=HD)
                        sp.dma_start(dst[hg][r * HD:(r + 1) * HD, :, :], rows).then_inc(qk_loaded[hg], 16)
                vr = vd[seq, HG * HD * hg:HG * HD * (hg + 1)].rearrange("(t p) d -> p t d", p=P)
                sp.dma_start(v_raw[hg % 2][:], vr).then_inc(v_loaded[hg % 2], 16)

            def store_max(n, slot):
                sp.wait_ge(nmt_ready, n + 2)
                for part in range(PARTS):
                    src = nmt[part * HG * QT:(part + 1) * HG * QT, :]
                    dst = qs[slot][STACK + part:STACK + part + 1, :, :].rearrange("a h (t q) -> a (h t) q", q=P)
                    sp.dma_start(dst, src).then_inc(nm_stored, 16)

            def store_o(n, bt, hg):
                wait_apart(sp, o_copied, n + 2, sp_passed)
                sp.dma_start(od[hg][:, bass.ds(SEQ * bt, SEQ)], oout[hg % 2][:]).then_inc(o_stored[hg % 2], 16)

            load(0, 0)
            load(0, 1)
            store_max(0, 0)

            def body(bt, hg, before, follow):
                n = HG * bt + hg
                if follow == 2:
                    if before:
                        wait_apart(sp, av_done, QT * n - 4, sp_passed)
                    wait_apart(sp, v_ready, n + 1, sp_passed)
                    load(bt + (hg + 2) // HG, (hg + 2) % HG)
                if before:
                    store_o(n - 1, *((bt, hg - 1) if hg else (bt - 1, HG - 1)))
                if follow:
                    store_max(n + 1, (hg + 1) % HG)

            groups(sp, body)
            store_o(N_GROUPS - 1, BATCH - 1, HG - 1)
            for u in range(2):
                sp.wait_ge(o_stored[u], 16 * (N_GROUPS // 2 + 1))

        @block.gpsimd
        def _(pool):
            pool.sem_inc(masked, 1)
            nc.gpsimd.memset(identb[:], 0.0)
            nc.gpsimd.memset(maskb[:], 0.0)
            for u in range(2):
                i = nc.gpsimd.memset(va[u][:, :, :, HD:2 * HD], 1.0)
            i.then_inc(cleared, 1)
            pool.wait_ge(cleared, 1)
            nc.gpsimd.affine_select(out=identb[:], in_=identb[:], compare_op=ALU.not_equal, fill=1.0,
                                    base=0, pattern=[[-1, P]], channel_multiplier=1)
            nc.gpsimd.affine_select(out=maskb[:], in_=maskb[:], compare_op=ALU.is_ge, fill=NEG,
                                    base=0, pattern=[[-1, P]], channel_multiplier=1).then_inc(consts, 1)

            def augment(n, u, nth):
                wait_apart(pool, v_loaded[u], 16 * nth, pool_passed)
                nc.gpsimd.tensor_copy(va[u][:, :, :, 0:HD], v_raw[u][:].rearrange("p t (h d) -> p t h d", d=HD)).then_inc(v_ready, 1)

            augment(0, 0, 1)
            pool.wait_ge(v_ready, 1)
            for s in range(HG):
                nc.gpsimd.memset(ks[s][STACK:ROWS, :, :], 1.0).then_inc(k_ones, 1)
                pool.wait_ge(k_ones, s + 1)

            def body(bt, hg, before, follow):
                n = HG * bt + hg
                for kt in range(QT):
                    wait_apart(pool, exp_done, NU * n + LAST_OF[kt] + 3, pool_passed)
                    diag = prob[kt % 2][:, :, kt * P:(kt + 1) * P]
                    nc.gpsimd.affine_select(out=diag, in_=diag, compare_op=ALU.is_ge, fill=0.0, base=0,
                                            pattern=[[0, HG], [1, P]], channel_multiplier=-1).then_inc(masked, 1)
                    if kt == 2 and follow:
                        wait_apart(pool, av_done, QT * n + 2, pool_passed)
                        augment(n + 1, (hg + 1) % 2, 2 * bt + (hg + 1) // 2 + 1)

            groups(pool, body)

        @block.scalar
        def _(act):
            act.preload_act_table(ACT.Exp)
            act.sem_inc(exp_done, 2)
            act.sem_inc(o_copied, 1)
            for u in range(2):
                act.sem_inc(o_stored[u], 16)

            def body(bt, hg, before, follow):
                n = HG * bt + hg
                for unit, (kt, j, heads) in enumerate(UNITS):
                    act.wait_ge(st_done, NU * n + unit + 1)
                    if unit == FIRST_OF[kt]:
                        act.wait_ge(av_done, QT * n + kt + 1)
                    nc.scalar.activation(prob[kt % 2][:, j:j + heads, kt * P:SEQ], unit_ps(unit), ACT.Exp).then_inc(exp_done, 1)
                    if unit == HG - 1 and before:
                        copy_o(n - 1, (hg + 1) % 2, 2 * bt + (hg + 1) // 2)

            def copy_o(n, u, nth):
                act.wait_ge(av_done, QT * n + QT + 2)
                act.wait_ge(o_stored[u], 16 * nth)
                nc.scalar.activation(oout[u][:], o_ps[:], ACT.Copy).then_inc(o_copied, 1)

            groups(act, body)
            copy_o(N_GROUPS - 1, 1, N_GROUPS // 2)

        @block.vector
        def _(dve):
            dve.sem_inc(piece_maxed, 2)
            dve.sem_inc(nmt_ready, 1)
            dve.sem_inc(nm_stored, 16)

            def piece_max(n, hg, p):
                qt, half, j, heads, keys = PIECES[p]
                dve.wait_ge(piece_done, NP * n + p + 1)
                nc.vector.reduce_max(mx[hg % 2][:, half, j:j + heads, qt], piece_ps(hg, p), AX_X).then_inc(piece_maxed, 1)

            def negate_step(n, hg, step):
                u = hg % 2
                m = mx[u][:, 0, :, :].rearrange("p h t -> p (h t)")
                if step == 0:
                    dve.wait_ge(piece_maxed, NP * (n + 1) + 2)
                    nc.vector.tensor_tensor(mx[u][:, 0, :, QT // 2:QT], mx[u][:, 0, :, QT // 2:QT],
                                            mx[u][:, 1, :, QT // 2:QT], ALU.max).then_inc(m_chain, 1)
                    return
                dve.wait_ge(m_chain, (CHAIN - 1) * n + step)
                if step == 1:
                    dve.wait_ge(nmt_done, n + 1)
                    nc.vector.tensor_scalar(nm[:, 0, :], m, -1.0, None, ALU.mult).then_inc(m_chain, 1)
                elif step == 2:
                    nc.vector.scalar_tensor_tensor(rest[:], m, -1.0, nm[:, 0, :], ALU.mult, ALU.subtract).then_inc(m_chain, 1)
                elif step == 3:
                    nc.vector.tensor_copy(nm[:, 1, :], rest[:]).then_inc(m_chain, 1)
                else:
                    nc.vector.tensor_tensor(nm[:, 2, :], rest[:], nm[:, 1, :], ALU.subtract).then_inc(nm_ready, 1)

            def copy_turned(n, hg):
                dve.wait_ge(nmt_done, n + 2)
                dve.wait_ge(nm_stored, 16 * PARTS * n + 16)
                nc.vector.tensor_copy(nmt[:], turned(hg)).then_inc(nmt_ready, 1)

            def early(n, hg, more):
                for p in range(EARLY):
                    if p == TURN:
                        copy_turned(n, hg)
                    if more:
                        piece_max(n + 1, hg + 1, p)
                    if p < CHAIN:
                        negate_step(n, hg, p)

            for p in range(NP):
                piece_max(0, 0, p)
            early(0, 0, True)

            def body(bt, hg, before, follow):
                if follow:
                    n = HG * bt + hg
                    for p in range(EARLY, NP):
                        piece_max(n + 1, hg + 1, p)
                    early(n + 1, hg + 1, follow == 2)

            groups(dve, body)

        @block.tensor
        def _(pe):
            pe.sem_inc(av_done, 2)
            pe.sem_inc(nmt_done, 1)

            def piece(n, hg, p):
                qt, half, first, heads, keys = PIECES[p]
                diagonal = qt // HG == half
                to = piece_ps(hg, p)
                if p == TURN + 1:
                    pe.wait_ge(nmt_ready, n + 1)
                pe.wait_ge(piece_maxed, NP * n + p + (2 if p == TURN else 1))
                for j in range(heads):
                    i = nc.tensor.matmul(to[:, j, :], qs[hg % HG][0:STACK, first + j, qt * P:(qt + 1) * P],
                                         ks[hg % HG][0:STACK, first + j, half * BANK:half * BANK + keys], start=True, stop=not diagonal)
                    if diagonal:
                        i = nc.tensor.matmul(to[:, j, keys - P:keys], identb[:], maskb[:], start=False, stop=True)
                i.then_inc(piece_done, 1)

            def transpose_max(n, hg, more):
                pe.wait_ge(nm_ready, n + 1)
                if more:
                    pe.wait_ge(piece_maxed, NP * (n + 1) + TURN + 1)
                nc.tensor.transpose(turned(hg), nm[:].rearrange("p a m -> p (a m)"), identb[:]).then_inc(nmt_done, 1)

            def search(bt, hg, p, follow):
                n = HG * bt + hg
                if p < NP:
                    piece(n + 1, hg + 1, p)
                    return
                if p - NP == TURN:
                    transpose_max(n + 1, hg + 1, follow == 2)
                if follow == 2:
                    if p == NP:
                        pe.wait_ge(qk_loaded[(hg + 2) % HG], 12 * 16 * (bt + (hg + 2) // HG + 1))
                    piece(n + 2, hg + 2, p - NP)

            pe.wait_ge(consts, 1)
            pe.wait_ge(qk_loaded[0], 12 * 16)
            for p in range(NP):
                piece(0, 0, p)
            pe.wait_ge(qk_loaded[1], 12 * 16)
            for p in range(EARLY):
                if p == TURN:
                    transpose_max(0, 0, True)
                piece(1, 1, p)
            pe.wait_ge(k_ones, HG)

            def body(bt, hg, before, follow):
                n = HG * bt + hg
                turns = range(EARLY, NP + EARLY)
                turn = 0
                now = dve_free = act_free = 0
                bank_free, unit_free = [0, 0], [0, 0]

                def pace(cols):
                    nonlocal now, turn, dve_free
                    now += cols
                    while follow and turn < len(turns) and bank_free[0] <= now:
                        p = turns[turn]
                        search(bt, hg, p, follow)
                        qt, half, _, heads, keys = PIECES[p % NP]
                        now += heads * (keys + (P if qt // HG == half else 0)) + (P if p == NP + TURN else 0)
                        dve_free = max(dve_free, now + TO_OTHER) + DVE_COLUMN * heads * keys + DVE_START
                        if NP <= p < NP + CHAIN or p == NP + TURN:
                            dve_free += DVE_START + P
                        bank_free[:] = bank_free[1], dve_free + TO_TENSOR
                        turn += 1

                def scores(unit):
                    nonlocal now, act_free
                    kt, first, heads = UNITS[unit]
                    while now < unit_free[0]:
                        pace(P)
                    if unit == 0:
                        pe.wait_ge(nm_stored, 16 * PARTS * (n + 1) + 16)
                    pe.wait_ge(exp_done, NU * n + unit + 1)
                    to = unit_ps(unit)
                    for j in range(first, first + heads):
                        for lo, hi in segments(kt):
                            i = nc.tensor.matmul(to[:, j - first, lo - kt * P:hi - kt * P],
                                                 ks[hg][0:ROWS, j, kt * P:(kt + 1) * P],
                                                 qs[hg][0:ROWS, j, lo:hi], start=True, stop=True)
                            if (j, hi) == (first + heads - 1, SEQ):
                                i.then_inc(st_done, 1)
                            pace(hi - lo)
                    act_free = max(act_free, now + TO_OTHER) + ACT_COLUMN * heads * (SEQ - P * kt) + ACT_START
                    unit_free[:] = unit_free[1], act_free + TO_TENSOR

                def values(n, kt, u, some=slice(None)):
                    for lo, hi in segments(kt)[some]:
                        if lo == kt * P:
                            pe.wait_ge(masked, QT * n + kt + 2)
                            if kt == 0:
                                pe.wait_ge(v_ready, n + 1)
                                pe.wait_ge(o_copied, n + 1)
                        for j in range(HG):
                            i = nc.tensor.matmul(o_ps[2 * HD * j:2 * HD * (j + 1), lo:hi], va[u][:, kt, j, :],
                                                 prob[kt % 2][:, j, lo:hi], start=(kt == 0), stop=(kt * P + P == hi))
                        if hi == SEQ:
                            i.then_inc(av_done, 1)
                        pace(HG * (hi - lo) + P)

                for unit, (kt, first, heads) in enumerate(UNITS):
                    scores(unit)
                    if unit == 1 and before:
                        values(n - 1, QT - 1, (hg + 1) % 2)
                    if kt >= 1 and heads == 1 and first == 2:
                        values(n, kt - 1, hg % 2, slice(0, 1))
                    elif kt >= 1 and first + heads == HG:
                        values(n, kt - 1, hg % 2, slice(1 if heads == 1 else 0, None))
                if not follow:
                    values(n, QT - 1, hg % 2)
                pace(float("inf"))

            groups(pe, body)


def combine(nc, x, wout, out, scratch, keep):
    od, fd = scratch["o"], scratch["f"]
    ident = keep["ident"]
    N = TOK // P
    S = 8
    with ExitStack() as ctx:
        b = Bufs(nc, ctx)
        wo_raw = b.sb("c_wo_raw", [P, HALVES, DIM])
        woh = b.sb("c_woh", [P, HALVES, DIM], F32R)
        wol = b.sb("c_wol", [P, HALVES, DIM], F32R)
        ot = [b.sb(f"c_ot{s}", [P, HG, P]) for s in range(S)]
        f = [b.sb(f"c_f{s}", [P, DIM]) for s in range(S)]
        gate = [b.sb(f"c_gate{s}", [P, DIM]) for s in range(S)]
        xt = [b.sb(f"c_xt{s}", [P, DIM]) for s in range(S)]
        inv = [b.sb(f"c_inv{s}", [P, HEADS, 1]) for s in range(S)]
        on = [b.sb(f"c_on{s}", [P, HEADS, HD]) for s in range(S)]
        onh = [b.sb(f"c_onh{s}", [P, HALVES, P], F32R) for s in range(S)]
        onl = [b.sb(f"c_onl{s}", [P, HALVES, P], F32R) for s in range(S)]
        res = [b.sb(f"c_res{s}", [P, DIM]) for s in range(S)]
        t_ps = [b.ps(f"c_t_ps{u}", [P, HEADS, 2 * HD]) for u in range(2)]
        b_ps = [b.ps(f"c_b_ps{u}", [P, HALVES, P]) for u in range(2)]
        s_ps = [b.ps(f"c_s_ps{u}", [P, DIM]) for u in range(2)]

        w_loaded, w_high, w_split = b.sem("c_w_loaded"), b.sem("c_w_high"), b.sem("c_w_split")
        loaded = [b.sem(f"c_loaded{s}") for s in range(S)]
        heads_done, inv_done, divided, back_done = b.sem("c_heads_done"), b.sem("c_inv_done"), b.sem("c_divided"), b.sem("c_back_done")
        high_done, low_done, proj_done = b.sem("c_high_done"), b.sem("c_low_done"), b.sem("c_proj_done")
        gated, mixed, added = b.sem("c_gated"), b.sem("c_mixed"), b.sem("c_added")
        stored = [b.sem(f"c_stored{s}") for s in range(S)]

        block = ctx.enter_context(nc.Block())

        def steps(eng, lags, body):
            deepest = max(lags)

            def step(q, r):
                for k, lag in enumerate(lags):
                    i = S * q + r - lag
                    if isinstance(q, int) and not 0 <= i < N:
                        continue
                    body(k, i, (r - lag) % S, q + 1 + (r - lag) // S)

            assert deepest <= S
            for r in range(S):
                step(0, r)
            with eng.Fori(1, N // S) as q:
                for r in range(S):
                    step(q, r)
            for r in range(deepest):
                step(N // S, r)

        @block.sync
        def _(sp):
            sp.dma_start(wo_raw[:], wout.rearrange("(c p) n -> p c n", p=P)).then_inc(w_loaded, 16)

            def body(k, i, s, nth):
                tokens = bass.ds(P * i, P)
                if k == 0:
                    sp.wait_ge(added, i + 1)
                    sp.dma_start(ot[s][:], od[:, :, tokens].rearrange("h p n -> p h n")).then_inc(loaded[s], 16)
                    sp.dma_start(f[s][:], fd[tokens, :]).then_inc(loaded[s], 16)
                    sp.dma_start(xt[s][:], x[tokens, :]).then_inc(loaded[s], 16)
                else:
                    sp.wait_ge(added, i + S + 1)
                    sp.dma_start(out[tokens, :], res[s][:]).then_inc(stored[s], 16)

            steps(sp, (0, S - 1), body)
            for s in range(S):
                sp.wait_ge(stored[s], 16 * (N // S + 1))

        @block.gpsimd
        def _(pool):
            pool.sem_inc(added, S)

            def body(k, i, s, nth):
                pool.wait_ge(mixed, i + S + 1)
                nc.gpsimd.tensor_tensor(res[s][:], res[s][:], xt[s][:], ALU.add).then_inc(added, 1)

            steps(pool, (0,), body)

        @block.scalar
        def _(act):
            act.preload_act_table(ACT.Silu)
            for s in range(S):
                act.sem_inc(stored[s], 16)

            def body(k, i, s, nth):
                if k == 0:
                    act.wait_ge(loaded[s], 48 * nth)
                    act.wait_ge(mixed, i + 1)
                    nc.scalar.activation(gate[s][:], f[s][:], ACT.Silu).then_inc(gated, 1)
                else:
                    act.wait_ge(back_done, i + 1)
                    act.wait_ge(proj_done, i + 1)
                    nc.scalar.activation(onh[s][:], b_ps[s % 2][:], ACT.Copy).then_inc(high_done, 1)

            steps(act, (0, 1), body)

        @block.vector
        def _(dve):
            dve.sem_inc(divided, 2)
            dve.sem_inc(low_done, 2)
            dve.sem_inc(mixed, S)
            dve.wait_ge(w_loaded, 16)
            nc.vector.tensor_copy(woh[:], wo_raw[:]).then_inc(w_high, 1)
            dve.wait_ge(w_high, 1)
            nc.vector.tensor_tensor(wol[:], wo_raw[:], woh[:].bitcast(F32), ALU.subtract).then_inc(w_split, 1)

            def body(k, i, s, nth):
                if k == 0:
                    dve.wait_ge(heads_done, i + 1)
                    nc.vector.reciprocal(inv[s][:], t_ps[s % 2][:, :, HD:HD + 1]).then_inc(inv_done, 1)
                    dve.wait_ge(inv_done, i + 1)
                    nc.vector.tensor_tensor(on[s][:], t_ps[s % 2][:, :, 0:HD], inv[s][:].broadcast_to([P, HEADS, HD]),
                                            ALU.mult).then_inc(divided, 1)
                elif k == 1:
                    dve.wait_ge(high_done, i + 1)
                    nc.vector.tensor_tensor(onl[s][:], b_ps[s % 2][:], onh[s][:].bitcast(F32), ALU.subtract).then_inc(low_done, 1)
                else:
                    dve.wait_ge(proj_done, i + S + 1)
                    dve.wait_ge(gated, i + 1)
                    dve.wait_ge(stored[s], 16 * nth)
                    nc.vector.tensor_tensor(res[s][:], s_ps[s % 2][:], gate[s][:], ALU.mult).then_inc(mixed, 1)

            steps(dve, (0, 1, 2), body)

        @block.tensor
        def _(pe):
            pe.sem_inc(proj_done, S)
            pe.wait_ge(w_split, 1)

            def body(k, i, s, nth):
                u = s % 2
                if k == 0:
                    pe.wait_ge(loaded[s], 48 * nth)
                    pe.wait_ge(divided, i + 1)
                    for h in range(HG):
                        n = nc.tensor.transpose(t_ps[u][:, h * HG:(h + 1) * HG, :], ot[s][:, h, :], ident[:])
                    n.then_inc(heads_done, 1)
                elif k == 1:
                    pe.wait_ge(divided, i + 3)
                    pe.wait_ge(low_done, i + 1)
                    for c in range(HALVES):
                        n = nc.tensor.transpose(b_ps[u][:, c, :], on[s][:, c * P // HD:(c + 1) * P // HD, :].rearrange("p h d -> p (h d)"), ident[:])
                    n.then_inc(back_done, 1)
                else:
                    pe.wait_ge(low_done, i + 3)
                    pe.wait_ge(mixed, i + S - 1)
                    for c in range(HALVES):
                        for t, w in ((onh, woh), (onh, wol), (onl, woh)):
                            n = nc.tensor.matmul(s_ps[u][:], t[s][:, c, :], w[:, c, :],
                                                 start=(c == 0 and t is onh and w is woh), stop=(c == HALVES - 1 and t is onl))
                    n.then_inc(proj_done, 1)

            steps(pe, (0, 1, 2), body)


def gated_block(nc, x, wqkv, wout, w1t, b1, w2t, b2, ln_g, ln_b, out):
    scratch = {
        "q": nc.dram_tensor("q_parts", [DIM, PARTS, TOK], BF16, kind="Internal").ap(),
        "k": nc.dram_tensor("k_parts", [DIM, PARTS, TOK], BF16, kind="Internal").ap(),
        "v": nc.dram_tensor("values", [TOK, DIM], F32, kind="Internal").ap(),
        "f": nc.dram_tensor("mlp_out", [TOK, DIM], F32, kind="Internal").ap(),
        "o": nc.dram_tensor("attention_t", [HG, P, TOK], F32, kind="Internal").ap(),
    }
    with ExitStack() as ctx:
        b = Bufs(nc, ctx)
        keep = {"ident": b.sb("ident", [P, P]), "mhalf": b.sb("mhalf", [P, TILES])}
        with ExitStack() as inner:
            b = Bufs(nc, inner)
            keep |= {
                "xth": b.sb("xth", [P, HALVES, TOK], F32R),
                "xtl": b.sb("xtl", [P, HALVES, TOK], F32R),
                "xres": b.sb("xres", [P, TOK // P, DIM]),
                "y": [b.sb(f"y{u}", [P, TILES, DIM]) for u in range(2)],
            }
            project(nc, x, wqkv, scratch, keep)
            mlp(nc, w1t, w2t, b1, b2, ln_g, ln_b, scratch, keep)
        attend(nc, scratch)
        combine(nc, x, wout, out, scratch, keep)


def kernel(L0_attn_x, L0_attn_w_qkv, L0_attn_w_out, L0_ffn_W1, L0_ffn_B1, L0_ffn_W2, L0_ffn_B2, L0_ffn_LN_G, L0_ffn_LN_B):
    import numpy as np
    import concourse.bacc as bacc
    from concourse.bass_utils import run_bass_kernel_spmd

    nc = bacc.Bacc("TRN2", target_bir_lowering=False, num_devices=1)
    arrays = {
        "x": np.asarray(L0_attn_x).reshape(TOK, DIM),
        "w_qkv": np.asarray(L0_attn_w_qkv),
        "w_out": np.asarray(L0_attn_w_out),
        "w1t": np.asarray(L0_ffn_W1).transpose(0, 2, 1),
        "b1": np.asarray(L0_ffn_B1).reshape(BLOCKS, CH, P).transpose(0, 2, 1),
        "w2t": np.asarray(L0_ffn_W2).transpose(0, 2, 1),
        "b2": np.asarray(L0_ffn_B2),
        "ln_g": np.asarray(L0_ffn_LN_G),
        "ln_b": np.asarray(L0_ffn_LN_B),
    }
    arrays = {k: np.ascontiguousarray(v) for k, v in arrays.items()}
    args = [nc.dram_tensor(k, v.shape, mybir.dt.from_np(v.dtype), kind="ExternalInput").ap() for k, v in arrays.items()]
    out = nc.dram_tensor("out", [TOK, DIM], F32, kind="ExternalOutput").ap()
    gated_block(nc, *args, out)
    r = run_bass_kernel_spmd(nc, [arrays], core_ids=[0])
    return r.results[0]["out"].reshape(BATCH, SEQ, DIM)
```

```python
from contextlib import ExitStack

import concourse.bass as bass
from concourse import mybir

F32 = mybir.dt.float32
F32R = mybir.dt.float32r
BF16 = mybir.dt.bfloat16
ALU = mybir.AluOpType
ACT = mybir.ActivationFunctionType
AX_X = mybir.AxisListType.X

P = 128
BATCH, SEQ, DIM = 4, 1024, 256
TOK = BATCH * SEQ
HEADS, HD = 16, 16
HALVES = DIM // P
GT = 512
TILES = GT // P
GROUPS = TOK // GT
PAIRS = GROUPS // 2
BLOCKS = 6
HID = 4 * DIM
CH = HID // P
EPS = 1e-5
HG = 4
QT = SEQ // P
BANK = 512
PARTS = 3
STACK = 6 * HD
ROWS = STACK + PARTS
EARLY = 10
TURN = 6
DVE_COLUMN, DVE_START = 2.5, 150
ACT_COLUMN, ACT_START = 2.0, 500
TO_OTHER, TO_TENSOR = 600, 380
LOADS = 12
OUT_DMAS = HG
OT = 4
NEG = -1.0e30


class Bufs:

    def __init__(self, nc, ctx):
        self.nc, self.ctx = nc, ctx

    def sb(self, name, shape, dt=F32):
        return self.ctx.enter_context(self.nc.sbuf_tensor(name, shape, dt))

    def ps(self, name, shape, dt=F32):
        return self.ctx.enter_context(self.nc.psum_tensor(name, shape, dt))

    def sem(self, name):
        return self.ctx.enter_context(self.nc.semaphore(name))


def wait_apart(eng, sem, value, passed):
    eng.wait_ge(sem, value)
    eng.sem_inc(passed, 1)


def max_pieces():
    pieces = []
    for qt in range(QT):
        for half in range(1 + qt // HG):
            keys = min(P * (qt + 1) - BANK * half, BANK)
            heads = min(BANK // keys, HG)
            pieces += [(qt, half, j, heads, keys) for j in range(0, HG, heads)]
    return pieces


def load_stacks(sp, scratch, to_q, to_k, bt, hg, loaded):
    for to, src, order in ((to_q, scratch["q"], (0, 0, 0, 1, 1, 2)), (to_k, scratch["k"], (0, 1, 2, 0, 1, 0))):
        for r, part in enumerate(order):
            rows = src[HG * HD * hg:HG * HD * (hg + 1), part, bass.ds(SEQ * bt, SEQ)].rearrange("(h d) n -> d h n", d=HD)
            sp.dma_start(to[r * HD:(r + 1) * HD, :, :], rows).then_inc(loaded, 16)


def shared_stacks(keep):
    views = [w[:].bitcast(BF16).rearrange("p (h n) -> p h n", n=SEQ) for w in keep["shared"]]
    return views[0:2], views[2:4]


def piece_products(nc, to, q, k, piece, keep):
    qt, half, first, heads, keys = piece
    diagonal = qt // HG == half
    for j in range(heads):
        i = nc.tensor.matmul(to[:, j, :], q[0:STACK, first + j, qt * P:(qt + 1) * P],
                             k[0:STACK, first + j, half * BANK:half * BANK + keys], start=True, stop=not diagonal)
        if diagonal:
            i = nc.tensor.matmul(to[:, j, keys - P:keys], keep["identb"][:], keep["maskb"][:], start=False, stop=True)
    return i


def by_head(bank, piece):
    _, _, _, heads, keys = piece
    return bank[:, 0:heads * keys].rearrange("p (h n) -> p h n", n=keys)


def row_max(nc, mx, scores, piece):
    qt, half, first, heads, _ = piece
    return nc.vector.reduce_max(mx[:, half, first:first + heads, qt], scores, AX_X)


def project(nc, x, wqkv, scratch, keep):
    qd, kd, vd = scratch["q"], scratch["k"], scratch["v"]
    xth, xtl, xres, y, ident = keep["xth"], keep["xtl"], keep["xres"], keep["y"], keep["ident"]
    with ExitStack() as ctx:
        b = Bufs(nc, ctx)
        xin = [b.sb(f"p_xin{u}", [P, TILES, DIM]) for u in range(2)]
        w_raw = b.sb("p_w_raw", [P, HALVES, 3 * DIM])
        wh, wl = (keep["shared"][n][:, 0:HALVES * 3 * DIM].rearrange("p (c n) -> p c n", c=HALVES) for n in range(2))
        gth = [b.sb(f"p_gth{u}", [P, HALVES, GT], F32R) for u in range(2)]
        gtl = [b.sb(f"p_gtl{u}", [P, HALVES, GT], F32R) for u in range(2)]
        part = [b.sb(f"p_part{m}", [P, PARTS, GT], BF16) for m in range(4)]
        rest = [b.sb(f"p_rest{m}", [P, GT]) for m in range(4)]
        vout = [b.sb(f"p_vout{u}", [P, TILES, DIM]) for u in range(2)]
        stats = [b.sb(f"p_stats{u}", [P, TILES, 6]) for u in range(2)]
        mv = [b.sb(f"p_mv{u}", [P, TILES, 2]) for u in range(2)]
        var = [b.sb(f"p_var{u}", [P, TILES]) for u in range(2)]
        rstd = [b.sb(f"p_rstd{u}", [P, TILES]) for u in range(2)]
        tr_ps = b.ps("p_tr_ps", [P, HALVES, GT])
        qk_ps = [b.ps(f"p_qk_ps{m}", [P, GT]) for m in range(4)]
        v_ps = b.ps("p_v_ps", [P, TILES, DIM])

        w_loaded, w_high, w_split = b.sem("p_w_loaded"), b.sem("p_w_high"), b.sem("p_w_split")
        x_loaded = [b.sem(f"p_x_loaded{u}") for u in range(2)]
        stats_done, mean_done, var_ready = b.sem("p_stats_done"), b.sem("p_mean_done"), b.sem("p_var_ready")
        rstd_ready, normed = b.sem("p_rstd_ready"), b.sem("p_normed")
        xres_done, xth_done = b.sem("p_xres_done"), b.sem("p_xth_done")
        gtl_stored = [b.sem(f"p_gtl_stored{u}") for u in range(2)]
        transposed, high_done, low_done = b.sem("p_transposed"), b.sem("p_high_done"), b.sem("p_low_done")
        qk_done, part0_done, rest_done = b.sem("p_qk_done"), b.sem("p_part0_done"), b.sem("p_rest_done")
        part1_done, part2_done = b.sem("p_part1_done"), b.sem("p_part2_done")
        part_stored = [b.sem(f"p_part_stored{m}") for m in range(4)]
        v_done, v_copied = b.sem("p_v_done"), b.sem("p_v_copied")
        v_stored = [b.sem(f"p_v_stored{u}") for u in range(2)]
        ident_ready = b.sem("p_ident_ready")
        half_ready, passed = b.sem("p_half_ready"), b.sem("p_passed")
        sp_passed = b.sem("p_sp_passed")

        block = ctx.enter_context(nc.Block())

        def pairs(eng, body):
            with eng.Fori(0, PAIRS - 1) as p:
                body(p, False)
            body(PAIRS - 1, True)

        @block.sync
        def _(sp):
            xg = x.rearrange("(g j p) d -> g p j d", p=P, j=TILES)

            def load_x(g, u):
                sp.dma_start(xin[u][:], xg[g]).then_inc(x_loaded[u], 16)

            load_x(0, 0)
            sp.dma_start(w_raw[:], wqkv.rearrange("(c p) n -> p c n", p=P)).then_inc(w_loaded, 16)
            load_x(1, 1)

            def keep_low(g, u):
                wait_apart(sp, low_done, g + 2, sp_passed)
                sp.dma_start(xtl[:, :, bass.ds(GT * g, GT)].bitcast(F32), gtl[u][:].bitcast(F32)).then_inc(gtl_stored[u], 16)

            def store(g, m):
                wait_apart(sp, part2_done, 4 * g + m + 5, sp_passed)
                rows = (qd if m < 2 else kd)[P * (m % 2):P * (m % 2) + P]
                sp.dma_start(rows[:, :, bass.ds(GT * g, GT)], part[m][:]).then_inc(part_stored[m], 16)

            sp.wait_ge(normed, 3)
            load_x(2, 0)
            keep_low(0, 0)

            def body(p, left):
                for u in range(2):
                    g = 2 * p + u
                    more = left > 0 or u == 0
                    if left > u:
                        wait_apart(sp, normed, g + 4, sp_passed)
                        load_x(g + 3, 1 - u)
                    store(g, 0)
                    if more:
                        keep_low(g + 1, 1 - u)
                    for m in range(1, 4):
                        store(g, m)
                    wait_apart(sp, v_copied, g + 2, sp_passed)
                    sp.dma_start(vd.rearrange("(g j p) d -> g p j d", p=P, j=TILES)[g], vout[u][:]).then_inc(v_stored[u], 16)

            with sp.Fori(0, PAIRS - 2) as p:
                body(p, 2)
            body(PAIRS - 2, 1)
            body(PAIRS - 1, 0)
            for u in range(2):
                sp.wait_ge(gtl_stored[u], 16 * (PAIRS + 1))
                sp.wait_ge(v_stored[u], 16 * (PAIRS + 1))
            for m in range(4):
                sp.wait_ge(part_stored[m], 16 * (GROUPS + 1))

        @block.gpsimd
        def _(pool):
            nc.gpsimd.memset(keep["identb"][:], 0.0)
            nc.gpsimd.memset(keep["maskb"][:], 0.0)
            nc.gpsimd.memset(ident[:], 0.0).then_inc(ident_ready, 1)
            nc.gpsimd.memset(keep["mhalf"][:], -0.5).then_inc(half_ready, 1)
            pool.wait_ge(ident_ready, 1)
            nc.gpsimd.affine_select(out=ident[:], in_=ident[:], compare_op=ALU.not_equal, fill=1.0,
                                    base=0, pattern=[[-1, P]], channel_multiplier=1).then_inc(ident_ready, 1)
            nc.gpsimd.affine_select(out=keep["identb"][:], in_=keep["identb"][:], compare_op=ALU.not_equal, fill=1.0,
                                    base=0, pattern=[[-1, P]], channel_multiplier=1).then_inc(half_ready, 1)
            pool.wait_ge(half_ready, 2)
            nc.gpsimd.affine_select(out=keep["maskb"][:], in_=keep["maskb"][:], compare_op=ALU.is_ge, fill=NEG,
                                    base=0, pattern=[[-1, P]], channel_multiplier=1).then_inc(half_ready, 1)
            pool.wait_ge(half_ready, 3)
            pool.sem_inc(part2_done, 4)

            def inverse(g, u):
                pool.wait_ge(var_ready, g + 1)
                nc.gpsimd.tensor_tensor(rstd[u][:], var[u][:], keep["mhalf"][:], ALU.pow).then_inc(rstd_ready, 1)

            def split_last(g, m):
                pool.wait_ge(part1_done, 4 * g + m + 1)
                nc.gpsimd.tensor_tensor(part[m][:, 2, :], rest[m][:], part[m][:, 1, :], ALU.subtract).then_inc(part2_done, 1)

            inverse(0, 0)
            inverse(1, 1)

            def body(p, last):
                for u in range(2):
                    g = 2 * p + u
                    for m in range(4):
                        split_last(g, m)
                        if m == 1 and not last:
                            inverse(g + 2, u)

            pairs(pool, body)

        @block.vector
        def _(dve):
            dve.sem_inc(normed, 2)
            dve.sem_inc(low_done, 1)
            dve.sem_inc(rest_done, 4)

            def statistics(g, u, n):
                dve.wait_ge(x_loaded[u], 16 * n)
                for j in range(TILES):
                    i = nc.vector.bn_stats(stats[u][:, j, :], xin[u][:, j, :])
                i.then_inc(stats_done, 1)
                wait_apart(dve, stats_done, g + 1, passed)
                for j in range(TILES):
                    i = nc.vector.bn_aggr(mv[u][:, j, :], stats[u][:, j, :])
                i.then_inc(mean_done, 1)
                dve.wait_ge(mean_done, g + 1)
                nc.vector.tensor_scalar(var[u][:], mv[u][:, :, 1], EPS, None, ALU.add).then_inc(var_ready, 1)

            def norm(g, u, n):
                dve.wait_ge(transposed, g + 1)
                dve.wait_ge(xres_done, g + 1)
                dve.wait_ge(rstd_ready, g + 1)
                for j in range(TILES):
                    i = nc.vector.tensor_scalar(y[u][:, j, :], xin[u][:, j, :], mv[u][:, j, 0:1],
                                                rstd[u][:, j:j + 1], ALU.subtract, ALU.mult)
                i.then_inc(normed, 1)

            def low(g, u, n):
                dve.wait_ge(high_done, g + 1)
                dve.wait_ge(v_done, g + 1)
                dve.wait_ge(gtl_stored[u], 16 * n)
                nc.vector.tensor_tensor(gtl[u][:], tr_ps[:], gth[u][:].bitcast(F32), ALU.subtract).then_inc(low_done, 1)

            def split_rest(g, m):
                dve.wait_ge(part0_done, 4 * g + m + 1)
                dve.wait_ge(part2_done, 4 * g + m + 1)
                nc.vector.scalar_tensor_tensor(rest[m][:], qk_ps[m][:], 0.25 if m < 2 else 1.0,
                                               part[m][:, 0, :], ALU.mult, ALU.subtract).then_inc(rest_done, 1)

            statistics(0, 0, 1)
            norm(0, 0, 1)
            dve.wait_ge(w_loaded, 16)
            nc.vector.tensor_copy(wh[:], w_raw[:]).then_inc(w_high, 1)
            low(0, 0, 1)
            dve.wait_ge(w_high, 1)
            nc.vector.tensor_tensor(wl[:], w_raw[:], wh[:].bitcast(F32), ALU.subtract).then_inc(w_split, 1)
            statistics(1, 1, 1)

            def body(p, last):
                for u in range(2):
                    g = 2 * p + u
                    more = not (last and u == 1)
                    if more:
                        norm(g + 1, 1 - u, p + 1 + u)
                    split_rest(g, 0)
                    split_rest(g, 1)
                    if not last:
                        statistics(g + 2, u, p + 2)
                    if more:
                        low(g + 1, 1 - u, p + 1 + u)
                    split_rest(g, 2)
                    split_rest(g, 3)

            pairs(dve, body)

        @block.scalar
        def _(act):
            act.sem_inc(v_copied, 1)
            act.sem_inc(xres_done, 2)
            act.sem_inc(xth_done, 2)
            for u in range(2):
                act.sem_inc(gtl_stored[u], 16)
                act.sem_inc(v_stored[u], 16)
            for m in range(4):
                act.sem_inc(part_stored[m], 16)

            def high(g, u):
                act.wait_ge(transposed, g + 3)
                act.wait_ge(v_done, g + 1)
                act.wait_ge(xth_done, g + 1)
                nc.scalar.activation(gth[u][:], tr_ps[:], ACT.Copy).then_inc(high_done, 1)

            def keep_high(g, u):
                act.wait_ge(high_done, g + 1)
                nc.scalar.activation(xth[:, :, bass.ds(GT * g, GT)], gth[u][:].bitcast(F32), ACT.Copy).then_inc(xth_done, 1)

            def keep_rows(g, u):
                act.wait_ge(normed, g + 3)
                nc.scalar.activation(xres[:, bass.ds(TILES * g, TILES), :], y[u][:], ACT.Copy).then_inc(xres_done, 1)

            def part0(g, m):
                act.wait_ge(qk_done, 4 * g + m + 1)
                act.wait_ge(part_stored[m], 16 * g + 16)
                nc.scalar.activation(part[m][:, 0, :], qk_ps[m][:], ACT.Copy,
                                     scale=0.25 if m < 2 else 1.0).then_inc(part0_done, 1)

            def part1(g, m):
                act.wait_ge(rest_done, 4 * g + m + 5)
                nc.scalar.activation(part[m][:, 1, :], rest[m][:], ACT.Copy).then_inc(part1_done, 1)

            keep_rows(0, 0)
            high(0, 0)
            keep_high(0, 0)

            def body(p, last):
                for u in range(2):
                    g = 2 * p + u
                    part0(g, 0)
                    part0(g, 1)
                    part1(g, 0)
                    if not (last and u == 1):
                        high(g + 1, 1 - u)
                    part1(g, 1)
                    part0(g, 2)
                    part0(g, 3)
                    if not (last and u == 1):
                        keep_high(g + 1, 1 - u)
                    part1(g, 2)
                    part1(g, 3)
                    if not (last and u == 1):
                        keep_rows(g + 1, 1 - u)
                    act.wait_ge(v_done, g + 3)
                    act.wait_ge(v_stored[u], 16 * p + 16)
                    nc.scalar.activation(vout[u][:], v_ps[:], ACT.Copy).then_inc(v_copied, 1)

            pairs(act, body)

        @block.tensor
        def _(pe):
            pe.sem_inc(transposed, 2)
            pe.sem_inc(v_done, 2)
            pe.wait_ge(ident_ready, 2)

            def transpose(g, u):
                pe.wait_ge(normed, g + 3)
                pe.wait_ge(low_done, g + 1)
                for c in range(HALVES):
                    for j in range(TILES):
                        i = nc.tensor.transpose(tr_ps[:, c, j * P:(j + 1) * P], y[u][:, j, c * P:(c + 1) * P], ident[:])
                i.then_inc(transposed, 1)

            transpose(0, 0)
            pe.wait_ge(w_split, 1)

            def body(p, last):
                for u in range(2):
                    g = 2 * p + u
                    pe.wait_ge(low_done, g + 2)
                    for m in range(4):
                        if m == 2 and not (last and u == 1):
                            transpose(g + 1, 1 - u)
                        pe.wait_ge(rest_done, 4 * g + m + 1)
                        cols = slice(P * m, P * m + P)
                        for c in range(HALVES):
                            for w, t in ((wh, gth), (wh, gtl), (wl, gth)):
                                i = nc.tensor.matmul(qk_ps[m][:], w[:, c, cols], t[u][:, c, :],
                                                     start=(c == 0 and w is wh and t is gth),
                                                     stop=(c == HALVES - 1 and w is wl))
                        i.then_inc(qk_done, 1)
                    pe.wait_ge(v_copied, g + 1)
                    for j in range(TILES):
                        for c in range(HALVES):
                            for t, w in ((gth, wh), (gth, wl), (gtl, wh)):
                                first = c == 0 and t is gth and w is wh
                                i = nc.tensor.matmul(v_ps[:, j, :], t[u][:, c, j * P:(j + 1) * P],
                                                     w[:, c, 2 * DIM:3 * DIM], start=(first and j % 2 == 0),
                                                     stop=(c == HALVES - 1 and t is gtl), skip_group_check=True)
                    i.then_inc(v_done, 1)

            pairs(pe, body)


def mlp(nc, w1t, w2t, b1, b2, ln_g, ln_b, scratch, keep):
    fd = scratch["f"]
    xth, xtl, xres, y, ident = keep["xth"], keep["xtl"], keep["xres"], keep["y"], keep["ident"]
    SLOTS = BLOCKS * GROUPS
    with ExitStack() as ctx:
        b = Bufs(nc, ctx)
        raw1 = [b.sb(f"m_raw1{u}", [P, HALVES, P]) for u in range(2)]
        raw2 = [b.sb(f"m_raw2{u}", [P, DIM]) for u in range(2)]
        w1h = [keep["shared"][0][:].rearrange("p (c n) -> p c n", c=HALVES), b.sb("m_w1h1", [P, HALVES, HID], F32R)]
        w1l = [keep["shared"][1][:].rearrange("p (c n) -> p c n", c=HALVES), b.sb("m_w1l1", [P, HALVES, HID], F32R)]
        w2h = [keep["shared"][2][:].rearrange("p (c n) -> p c n", c=CH), b.sb("m_w2h1", [P, CH, DIM], F32R)]
        w2l = [keep["shared"][3][:].rearrange("p (c n) -> p c n", c=CH), b.sb("m_w2l1", [P, CH, DIM], F32R)]
        b1s = [b.sb(f"m_b1s{u}", [P, CH]) for u in range(2)]
        b2s = [b.sb(f"m_b2s{u}", [P, 1, DIM]) for u in range(2)]
        lng = [b.sb(f"m_lng{u}", [P, DIM]) for u in range(2)]
        lnb = [b.sb(f"m_lnb{u}", [P, DIM]) for u in range(2)]
        hid = [b.sb(f"m_hid{k}", [P, GT]) for k in range(2)]
        hidh = [b.sb(f"m_hidh{k}", [P, GT], F32R) for k in range(4)]
        hidl = [b.sb(f"m_hidl{k}", [P, GT], F32R) for k in range(4)]
        stats = b.sb("m_stats", [P, TILES, 6])
        mv = b.sb("m_mv", [P, TILES, 2])
        var = b.sb("m_var", [P, TILES])
        rstd = b.sb("m_rstd", [P, TILES])
        h_ps = [b.ps(f"m_h_ps{k}", [P, GT]) for k in range(2)]
        y_ps = [b.ps(f"m_y_ps{u}", [P, TILES, DIM]) for u in range(2)]
        tr_ps = b.ps("m_tr_ps", [P, HALVES, GT])

        raw_loaded = [b.sem(f"m_raw_loaded{u}") for u in range(2)]
        bias_loaded = [b.sem(f"m_bias_loaded{u}") for u in range(2)]
        ln_loaded = [b.sem(f"m_ln_loaded{u}") for u in range(2)]
        w_high, w_split = b.sem("m_w_high"), b.sem("m_w_split")
        w1_done, gelu_done, low_done = b.sem("m_w1_done"), b.sem("m_gelu_done"), b.sem("m_low_done")
        w2_done, y_added, b2_added = b.sem("m_w2_done"), b.sem("m_y_added"), b.sem("m_b2_added")
        stats_done, mean_done, var_ready = b.sem("m_stats_done"), b.sem("m_mean_done"), b.sem("m_var_ready")
        rstd_ready, scaled, x_ready = b.sem("m_rstd_ready"), b.sem("m_scaled"), b.sem("m_x_ready")
        transposed, xth_done, xtl_done = b.sem("m_transposed"), b.sem("m_xth_done"), b.sem("m_xtl_done")
        xres_done, passed, last_added = b.sem("m_xres_done"), b.sem("m_passed"), b.sem("m_last_added")
        f_stored = [b.sem(f"m_f_stored{u}") for u in range(2)]
        stacks_loaded, piece_done, piece_maxed = b.sem("m_stacks_loaded"), b.sem("m_piece_done"), b.sem("m_piece_maxed")
        stacks = shared_stacks(keep)
        PIECES = max_pieces()

        block = ctx.enter_context(nc.Block())

        class Slot:

            def __init__(s, i, gp, u, par, nth, kind, first, searching=False):
                s.i, s.gp, s.u, s.par, s.nth, s.kind = i, gp, u, par, nth, kind
                s.g = 2 * gp + u
                s.t = GROUPS * i + s.g
                s.seam = first and u == 0
                s.start = kind == "first" and s.seam
                s.second = kind == "first" and first and u == 1
                s.epar = 1 - par if s.seam else par
                s.enth = nth - (1 - par) if s.seam else nth
                s.eg = GROUPS - 1 if s.seam else s.g - 1
                s.first = first
                s.final = kind == "last" and not s.seam
                s.more = kind != "last"
                s.searching = searching
                s.turning = not s.start and not s.second and (s.more or first)
                s.tg = GROUPS - 2 + u if first else s.g - 2

            def pieces(s, k, later):
                if not s.searching:
                    return range(0)
                step, steps = 2 * (CH * s.u + k) + later, 4 * CH
                return range(len(PIECES) * step // steps, len(PIECES) * (step + 1) // steps)

        def sweep(eng, slot, begin=None):
            def one(i, par, nth, kind):
                if begin:
                    begin(i, par, nth, kind)
                for u in range(2):
                    slot(Slot(i, 0, u, par, nth, kind, True))
                searching = kind == "last"
                with eng.Fori(1, PAIRS - 1 if searching else PAIRS) as gp:
                    for u in range(2):
                        slot(Slot(i, gp, u, par, nth, kind, False))
                if searching:
                    for u in range(2):
                        slot(Slot(i, PAIRS - 1, u, par, nth, kind, False, True))

            one(0, 0, 1, "first")
            with eng.Fori(0, (BLOCKS - 2) // 2) as q:
                one(2 * q + 1, 1, q + 1, "middle")
                one(2 * q + 2, 0, q + 2, "middle")
            one(BLOCKS - 1, 1, BLOCKS // 2, "last")

        @block.sync
        def _(sp):
            w1v = w1t.rearrange("i (c p) h -> i p c h", p=P)

            def load_raw(i, g, u):
                sp.dma_start(raw1[u][:], w1v[i][:, :, bass.ds(P * g, P)]).then_inc(raw_loaded[u], 16)
                sp.dma_start(raw2[u][:], w2t[i, bass.ds(P * g, P), :]).then_inc(raw_loaded[u], 16)

            def load_bias(i, par):
                sp.dma_start(b1s[par][:], b1[i]).then_inc(bias_loaded[par], 16)
                sp.dma_start(b2s[par][:, 0, :], b2[bass.ds(i, 1), :].broadcast_to([P, DIM])).then_inc(bias_loaded[par], 16)

            for g in range(GROUPS):
                if g >= 2:
                    sp.wait_ge(w_split, g - 1)
                load_raw(0, g, g % 2)
                if g == 0:
                    load_bias(0, 0)

            def begin(i, par, nth, kind):
                if kind == "last":
                    return
                if kind == "middle":
                    sp.wait_ge(x_ready, GROUPS * i - 7)
                sp.dma_start(lng[par][:], ln_g[bass.ds(i, 1), :].broadcast_to([P, DIM])).then_inc(ln_loaded[par], 16)
                sp.dma_start(lnb[par][:], ln_b[bass.ds(i, 1), :].broadcast_to([P, DIM])).then_inc(ln_loaded[par], 16)

            def slot(s):
                if s.more:
                    piece = GROUPS * (s.i + 1) + s.g
                    sp.wait_ge(w_split, piece - 1)
                    load_raw(s.i + 1, s.g, s.u)
                    if s.second or (s.kind == "middle" and s.first and s.u == 1):
                        if s.kind == "middle":
                            sp.wait_ge(b2_added, GROUPS * s.i)
                        load_bias(s.i + 1, 1 - s.par)
                if s.kind == "last" and s.first and s.u == 1:
                    sp.wait_ge(w2_done, CH * GROUPS * (BLOCKS - 1) + 4)
                    for hg in range(2):
                        load_stacks(sp, scratch, *stacks[hg], 0, hg, stacks_loaded)
                if s.final:
                    store_f(b2_added, s.t, s.eg, (s.u + 1) % 2)

            def store_f(added, count, eg, yu):
                sp.wait_ge(added, count)
                sp.dma_start(fd.rearrange("(g j p) d -> g p j d", p=P, j=TILES)[eg], y[yu][:]).then_inc(f_stored[yu], 16)

            sweep(sp, slot, begin)
            store_f(last_added, 1, GROUPS - 1, 1)
            for u in range(2):
                sp.wait_ge(f_stored[u], 16 * (PAIRS + 1))

        @block.gpsimd
        def _(pool):
            def slot(s):
                if not s.start:
                    add_b2(s.t, s.epar, 1 - s.u)
                    if not s.final:
                        pool.wait_ge(var_ready, s.t)
                        nc.gpsimd.tensor_tensor(rstd[:], var[:], keep["mhalf"][:], ALU.pow).then_inc(rstd_ready, 1)

            def add_b2(t, epar, yu):
                pool.wait_ge(y_added, t + 2)
                nc.gpsimd.tensor_tensor(y[yu][:], y[yu][:], b2s[epar][:].broadcast_to([P, TILES, DIM]),
                                        ALU.add).then_inc(b2_added, 1)

            def begin(i, par, nth, kind):
                pool.wait_ge(bias_loaded[par], 32 * nth)

            sweep(pool, slot, begin)

        @block.scalar
        def _(act):
            act.preload_act_table(ACT.Gelu)
            act.sem_inc(gelu_done, 2)
            act.sem_inc(xres_done, 1)
            for u in range(2):
                act.sem_inc(f_stored[u], 16)

            def begin(i, par, nth, kind):
                act.wait_ge(bias_loaded[par], 32 * nth)

            def slot(s):
                for k in range(CH):
                    n = CH * s.t + k
                    act.wait_ge(w1_done, n + 1)
                    act.wait_ge(low_done, n + 1)
                    nc.scalar.activation(hid[k % 2][:], h_ps[k % 2][:], ACT.Gelu, bias=b1s[s.par][:, k:k + 1])
                    act.wait_ge(w2_done, n + 1)
                    nc.scalar.activation(hidh[k % 4][:], h_ps[k % 2][:], ACT.Gelu, bias=b1s[s.par][:, k:k + 1]).then_inc(gelu_done, 1)
                    if k == 1 and s.turning:
                        act.wait_ge(transposed, s.t)
                        nc.scalar.activation(xth[:, :, bass.ds(GT * s.tg, GT)], tr_ps[:], ACT.Copy).then_inc(xth_done, 1)
                if s.start or s.final:
                    return
                act.wait_ge(x_ready, s.t + 1)
                nc.scalar.activation(xres[:, bass.ds(TILES * s.eg, TILES), :], y[1 - s.u][:], ACT.Copy).then_inc(xres_done, 1)

            sweep(act, slot, begin)

        @block.vector
        def _(dve):
            dve.sem_inc(low_done, 2)
            dve.sem_inc(y_added, 2)
            dve.sem_inc(xtl_done, 1)
            dve.sem_inc(x_ready, 1)

            def split_weights(i, g, u, par, nth):
                piece = GROUPS * i + g
                cols = bass.ds(P * g, P)
                dve.wait_ge(raw_loaded[u], 32 * nth)
                nc.vector.tensor_copy(w1h[par][:, :, cols], raw1[u][:])
                nc.vector.tensor_copy(w2h[par][:, bass.ds(g, 1), :].squeeze(1), raw2[u][:]).then_inc(w_high, 1)
                dve.wait_ge(w_high, piece + 1)
                nc.vector.tensor_tensor(w1l[par][:, :, cols], raw1[u][:], w1h[par][:, :, cols].bitcast(F32), ALU.subtract)
                nc.vector.tensor_tensor(w2l[par][:, bass.ds(g, 1), :].squeeze(1), raw2[u][:], w2h[par][:, bass.ds(g, 1), :].squeeze(1).bitcast(F32),
                                        ALU.subtract).then_inc(w_split, 1)

            for g in range(2):
                split_weights(0, g, g % 2, 0, 1)

            def add_y(t, eg, yu):
                dve.wait_ge(w2_done, CH * t + 4)
                nc.vector.tensor_tensor(y[yu][:], y_ps[yu][:], xres[:, bass.ds(TILES * eg, TILES), :],
                                        ALU.add).then_inc(y_added, 1)

            def piece_max(p):
                dve.wait_ge(piece_done, p + 1)
                row_max(nc, keep["mx"][0], by_head(tr_ps[:, p % 2, :], PIECES[p]), PIECES[p]).then_inc(piece_maxed, 1)

            def slot(s):
                epilogue = not (s.start or s.final)
                if not s.start:
                    if s.kind == "last" and not s.first:
                        dve.wait_ge(f_stored[1 - s.u], 16 * s.gp + 16 * s.u)
                        dve.wait_ge(transposed, GROUPS * (BLOCKS - 1) + 1)
                        dve.wait_ge(xres_done, GROUPS * (BLOCKS - 1) + 1)
                    elif not s.second:
                        dve.wait_ge(transposed, s.t - 1)
                        dve.wait_ge(xres_done, s.t - 1)
                    add_y(s.t, s.eg, 1 - s.u)
                yy = y[1 - s.u]
                for k in range(CH):
                    n = CH * s.t + k
                    for p in s.pieces(k, False):
                        piece_max(p)
                    dve.wait_ge(gelu_done, n + 3)
                    nc.vector.tensor_tensor(hidl[k % 4][:], hid[k % 2][:], hidh[k % 4][:].bitcast(F32),
                                            ALU.subtract).then_inc(low_done, 1)
                    for p in s.pieces(k, True):
                        piece_max(p)
                    if k == 1 and epilogue:
                        dve.wait_ge(b2_added, s.t)
                        for j in range(TILES):
                            i = nc.vector.bn_stats(stats[:, j, :], yy[:, j, :])
                        i.then_inc(stats_done, 1)
                    if k == 2 and s.turning:
                        cols = bass.ds(GT * s.tg, GT)
                        dve.wait_ge(xth_done, s.t - 1)
                        nc.vector.tensor_tensor(xtl[:, :, cols], tr_ps[:], xth[:, :, cols].bitcast(F32),
                                                ALU.subtract).then_inc(xtl_done, 1)
                    if k == 2 and epilogue:
                        wait_apart(dve, stats_done, s.t, passed)
                        for j in range(TILES):
                            i = nc.vector.bn_aggr(mv[:, j, :], stats[:, j, :])
                        i.then_inc(mean_done, 1)
                    if k == 3 and epilogue:
                        dve.wait_ge(mean_done, s.t)
                        nc.vector.tensor_scalar(var[:], mv[:, :, 1], EPS, None, ALU.add).then_inc(var_ready, 1)
                        dve.wait_ge(ln_loaded[s.epar], 32 * s.enth)
                        for j in range(TILES):
                            i = nc.vector.scalar_tensor_tensor(yy[:, j, :], yy[:, j, :], mv[:, j, 0:1], lng[s.epar][:],
                                                               ALU.subtract, ALU.mult)
                        i.then_inc(scaled, 1)
                    if s.start and k < GROUPS - 2:
                        split_weights(0, k + 2, k % 2, 0, k // 2 + 2)
                    if k == (7 if s.start else 4) and s.more:
                        split_weights(s.i + 1, s.g, s.u, 1 - s.par, 4 * (s.i + 1) + s.gp + 1)
                    if k == 5 and epilogue:
                        dve.wait_ge(scaled, s.t)
                        dve.wait_ge(rstd_ready, s.t)
                        for j in range(TILES):
                            i = nc.vector.scalar_tensor_tensor(yy[:, j, :], yy[:, j, :], rstd[:, j:j + 1], lnb[s.epar][:],
                                                               ALU.mult, ALU.add)
                        i.then_inc(x_ready, 1)

            sweep(dve, slot)
            dve.wait_ge(f_stored[1], 16 * PAIRS)
            add_y(SLOTS, GROUPS - 1, 1)
            dve.wait_ge(bias_loaded[1], 32 * (BLOCKS // 2))
            dve.wait_ge(y_added, SLOTS + 2)
            nc.vector.tensor_tensor(y[1][:], y[1][:], b2s[1][:].broadcast_to([P, TILES, DIM]), ALU.add).then_inc(last_added, 1)

        @block.tensor
        def _(pe):
            pe.sem_inc(w2_done, 4)
            pe.sem_inc(transposed, 1)

            def begin(i, par, nth, kind):
                if kind != "first":
                    pe.wait_ge(w_split, GROUPS * (i + 1))

            def slot(s):
                tokens = bass.ds(GT * s.g, GT)

                def up(k):
                    if s.start:
                        pe.wait_ge(w_split, k + 1)
                    pe.wait_ge(gelu_done, CH * s.t + k + 1)
                    for c in range(HALVES):
                        for w, x in ((w1h, xth), (w1h, xtl), (w1l, xth)):
                            i = nc.tensor.matmul(h_ps[k % 2][:], w[s.par][:, c, k * P:(k + 1) * P], x[:, c, tokens],
                                                 start=(c == 0 and w is w1h and x is xth), stop=(c == HALVES - 1 and w is w1l))
                    i.then_inc(w1_done, 1)

                def down(k):
                    pe.wait_ge(low_done, CH * s.t + k + 3)
                    if k == 0:
                        pe.wait_ge(y_added, s.t + 1)
                    for j in range(TILES):
                        for h, w in ((hidh, w2h), (hidh, w2l), (hidl, w2h)):
                            i = nc.tensor.matmul(y_ps[s.u][:, j, :], h[k % 4][:, j * P:(j + 1) * P], w[s.par][:, k, :],
                                                 start=(k == 0 and j % 2 == 0 and h is hidh and w is w2h),
                                                 stop=(k == CH - 1 and h is hidl), skip_group_check=True)
                    i.then_inc(w2_done, 1)

                def piece(p):
                    if p == 0:
                        pe.wait_ge(stacks_loaded, 2 * LOADS * 16)
                        pe.wait_ge(xtl_done, GROUPS * (BLOCKS - 1) + 1)
                    if p >= 2:
                        pe.wait_ge(piece_maxed, p - 1)
                    to = by_head(tr_ps[:, p % 2, :], PIECES[p])
                    piece_products(nc, to, *stacks[0], PIECES[p], keep).then_inc(piece_done, 1)

                if s.kind != "first":
                    pe.wait_ge(xtl_done, s.t - 6)
                def turn():
                    pe.wait_ge(x_ready, s.t)
                    pe.wait_ge(xtl_done, s.t - 1)
                    for c in range(HALVES):
                        for j in range(TILES):
                            i = nc.tensor.transpose(tr_ps[:, c, j * P:(j + 1) * P],
                                                    y[s.u][:, j, c * P:(c + 1) * P], ident[:])
                    i.then_inc(transposed, 1)

                for k in range(CH):
                    up(k)
                    if k == 1 and s.turning:
                        turn()
                    for p in s.pieces(k, False):
                        piece(p)
                    if k >= 2:
                        down(k - 2)
                    for p in s.pieces(k, True):
                        piece(p)
                down(CH - 2)
                down(CH - 1)

            sweep(pe, slot, begin)


def attention_steps():
    return [(half, kt, max(P * kt, BANK * half), BANK * (half + 1)) for half in range(2) for kt in range(HG * (half + 1))]


def score_units():
    units = []
    for step, (_, _, lo, hi) in enumerate(attention_steps()):
        heads = 2 if hi - lo > BANK // 2 else HG
        units += [(step, j, heads) for j in range(0, HG, heads)]
    return units


def attend(nc, x, wout, scratch, keep):
    vd, od = scratch["v"], scratch["o"]
    identb, mx = keep["identb"], keep["mx"]
    N_GROUPS = BATCH * HG
    PIECES = max_pieces()
    NP = len(PIECES)
    UNITS = score_units()
    NU = len(UNITS)
    CHAIN = 5
    STEPS = attention_steps()
    NS = len(STEPS)
    LAST_OF = [max(n for n, unit in enumerate(UNITS) if unit[0] == step) for step in range(NS)]
    FIRST_OF = [min(n for n, unit in enumerate(UNITS) if unit[0] == step) for step in range(NS)]
    LATE = 3
    DUE = [unit + LATE for unit in LAST_OF]
    BUFS = 3
    BANKS = 3
    with ExitStack() as ctx:
        b = Bufs(nc, ctx)
        qs = [stack[0] for stack in shared_stacks(keep)] + [b.sb(f"a_qs{s}", [P, HG, SEQ], BF16) for s in range(2, HG)]
        ks = [stack[1] for stack in shared_stacks(keep)] + [b.sb(f"a_ks{s}", [P, HG, SEQ], BF16) for s in range(2, HG)]
        v_raw = [b.sb(f"a_v_raw{u}", [P, QT, HG * HD]) for u in range(2)]
        va = [b.sb(f"a_va{u}", [P, QT, HG, 2 * HD]) for u in range(2)]
        prob = [b.sb(f"a_prob{u}", [P, HG, BANK]) for u in range(BUFS)]
        oout = [b.sb(f"a_oout{u}", [P, SEQ]) for u in range(2)]
        rest = b.sb("a_rest", [P, HG * QT])
        nm = b.sb("a_nm", [P, PARTS, HG * QT], BF16)
        ones = b.sb("a_ones", [PARTS, 1, SEQ], BF16)
        nmt = b.sb("a_nmt", [PARTS * HG * QT, P], BF16)
        st_ps = [b.ps(f"a_st_ps{u}", [P, SEQ]) for u in range(2)]
        s_ps = [b.ps(f"a_s_ps{u}", [P, BANK]) for u in range(BANKS)]
        o_ps = b.ps("a_o_ps", [P, BANK])

        qk_loaded = [b.sem(f"a_qk_loaded{s}") for s in range(HG)]
        v_loaded = [b.sem(f"a_v_loaded{u}") for u in range(2)]
        ones_ready, v_ones, v_ready = b.sem("a_ones_ready"), b.sem("a_v_ones"), b.sem("a_v_ready")
        k_ones = b.sem("a_k_ones")
        piece_done, piece_maxed = b.sem("a_piece_done"), b.sem("a_piece_maxed")
        m_chain, nm_ready, nmt_done, nmt_ready, nm_stored = b.sem("a_m_chain"), b.sem("a_nm_ready"), b.sem("a_nmt_done"), b.sem("a_nmt_ready"), b.sem("a_nm_stored")
        st_done, exp_done, masked, av_done = b.sem("a_st_done"), b.sem("a_exp_done"), b.sem("a_masked"), b.sem("a_av_done")
        o_copied, pool_passed, sp_passed = b.sem("a_o_copied"), b.sem("a_pool_passed"), b.sem("a_sp_passed")
        o_stored = [b.sem(f"a_o_stored{u}") for u in range(2)]

        block = ctx.enter_context(nc.Block())

        def unit_ps(unit):
            step, _, heads = UNITS[unit]
            _, _, lo, hi = STEPS[step]
            pitch = BANK if heads == 2 else hi - lo
            return st_ps[unit % 2][:, 0:heads * pitch].rearrange("p (h n) -> p h n", n=pitch)[:, :, 0:hi - lo]

        assert (NP + 1) % BANKS == 0

        def piece_ps(p):
            return by_head(s_ps[(p + (p >= TURN)) % BANKS], PIECES[p])

        turned = s_ps[TURN % BANKS][:].bitcast(BF16)[0:PARTS * HG * QT, 0:P]

        def groups(eng, body):
            for hg in range(HG):
                body(0, hg, hg > 0, 2)
            with eng.Fori(1, BATCH - 1) as bt:
                for hg in range(HG):
                    body(bt, hg, True, 2)
            for hg in range(HG):
                body(BATCH - 1, hg, True, min(2, HG - 1 - hg))

        @block.sync
        def _(sp):
            def load_values(bt, hg):
                seq = bass.ds(SEQ * bt, SEQ)
                vr = vd[seq, HG * HD * hg:HG * HD * (hg + 1)].rearrange("(t p) d -> p t d", p=P)
                sp.dma_start(v_raw[hg % 2][:], vr).then_inc(v_loaded[hg % 2], 16)

            def store_max(n, slot):
                sp.wait_ge(nmt_ready, n + 2)
                for part in range(PARTS):
                    src = nmt[part * HG * QT:(part + 1) * HG * QT, :]
                    dst = qs[slot][STACK + part:STACK + part + 1, :, :].rearrange("a h (t q) -> a (h t) q", q=P)
                    sp.dma_start(dst, src).then_inc(nm_stored, 16)

            def store_o(n, bt, hg):
                wait_apart(sp, o_copied, 2 * n + 3, sp_passed)
                for j in range(HG):
                    sp.dma_start(od[hg, j, :, bass.ds(SEQ * bt, SEQ)],
                                 oout[hg % 2][2 * HD * j:2 * HD * j + HD + 1, :]).then_inc(o_stored[hg % 2], 16)

            for hg in range(2):
                sp.sem_inc(qk_loaded[hg], LOADS * 16)
                load_values(0, hg)
            store_max(0, 0)

            def load_rows(n):
                tokens = bass.ds(TOK // N_GROUPS * n, TOK // N_GROUPS)
                tiles = bass.ds(QT // HG * n, QT // HG)
                for to, rows in (("x", x), ("f", scratch["f"])):
                    sp.dma_start(keep[to][:, tiles, :], rows[tokens, :].rearrange("(t p) d -> p t d", p=P)).then_inc(keep["rows_loaded"], 16)

            def body(bt, hg, before, follow):
                n = HG * bt + hg
                if follow == 2:
                    if before:
                        wait_apart(sp, av_done, NS * n - 4, sp_passed)
                    wait_apart(sp, v_ready, n + 1, sp_passed)
                    load_stacks(sp, scratch, qs[(hg + 2) % HG], ks[(hg + 2) % HG], bt + (hg + 2) // HG, (hg + 2) % HG,
                                qk_loaded[(hg + 2) % HG])
                    load_values(bt + (hg + 2) // HG, (hg + 2) % HG)
                if before:
                    store_o(n - 1, *((bt, hg - 1) if hg else (bt - 1, HG - 1)))
                load_rows(n)
                if follow:
                    store_max(n + 1, (hg + 1) % HG)

            groups(sp, body)
            for u in range(2):
                sp.wait_ge(o_stored[u], 16 * OUT_DMAS * (1 + HG // 2))
            sp.dma_start(keep["wo"][:], wout.rearrange("(c p) n -> p c n", p=P)).then_inc(keep["wo_loaded"], 16)
            for c in range(OT):
                load_pair(sp, od, keep, 2 * c, c)
            store_o(N_GROUPS - 1, BATCH - 1, HG - 1)
            sp.wait_ge(keep["rows_loaded"], 2 * 16 * N_GROUPS)
            for u in range(2):
                sp.wait_ge(o_stored[u], 16 * OUT_DMAS * (N_GROUPS // 2 + 1))

        @block.gpsimd
        def _(pool):
            pool.sem_inc(masked, 1)
            nc.gpsimd.memset(ones[:], 1.0).then_inc(ones_ready, 1)
            for u in range(2):
                nc.gpsimd.memset(va[u][:, :, :, HD:2 * HD], 1.0).then_inc(v_ones, 1)
                pool.wait_ge(v_ones, u + 1)

            def augment(n, u, nth):
                wait_apart(pool, v_loaded[u], 16 * nth, pool_passed)
                nc.gpsimd.tensor_copy(va[u][:, :, :, 0:HD], v_raw[u][:].rearrange("p t (h d) -> p t h d", d=HD)).then_inc(v_ready, 1)

            augment(0, 0, 1)

            def body(bt, hg, before, follow):
                n = HG * bt + hg
                for step, (half, kt, _, _) in enumerate(STEPS):
                    if kt // HG == half:
                        wait_apart(pool, exp_done, NU * n + LAST_OF[step] + 3, pool_passed)
                        diag = prob[step % BUFS][:, :, 0:P]
                        nc.gpsimd.affine_select(out=diag, in_=diag, compare_op=ALU.is_ge, fill=0.0, base=0,
                                                pattern=[[0, HG], [1, P]], channel_multiplier=-1).then_inc(masked, 1)
                    if step == HG and follow:
                        wait_apart(pool, av_done, NS * n + BUFS, pool_passed)
                        augment(n + 1, (hg + 1) % 2, 2 * bt + (hg + 1) // 2 + 1)

            groups(pool, body)

        @block.scalar
        def _(act):
            act.preload_act_table(ACT.Exp)
            act.wait_ge(ones_ready, 1)
            for s in range(HG):
                act.dma_start(ks[s][STACK:ROWS, :, :], ones[:].broadcast_to([PARTS, HG, SEQ])).then_inc(k_ones, 16)
            act.sem_inc(exp_done, 2)
            act.sem_inc(o_copied, 1)
            for u in range(2):
                act.sem_inc(o_stored[u], 16 * OUT_DMAS)

            def body(bt, hg, before, follow):
                n = HG * bt + hg
                for unit, (step, j, heads) in enumerate(UNITS):
                    _, _, lo, hi = STEPS[step]
                    act.wait_ge(st_done, NU * n + unit + 1)
                    if unit == FIRST_OF[step]:
                        act.wait_ge(av_done, NS * n + step + 1)
                    nc.scalar.activation(prob[step % BUFS][:, j:j + heads, 0:hi - lo], unit_ps(unit), ACT.Exp).then_inc(exp_done, 1)
                    if unit == DUE[NS - 1] - NU and before:
                        copy_o(n - 1, 1, (hg + 1) % 2, 2 * bt + (hg + 1) // 2)
                    if unit == DUE[HG - 1]:
                        copy_o(n, 0, hg % 2, 2 * bt + hg // 2 + 1)

            def copy_o(n, half, u, nth):
                act.wait_ge(av_done, NS * n + (NS if half else HG) + BUFS)
                if half == 0:
                    act.wait_ge(o_stored[u], 16 * OUT_DMAS * nth)
                nc.scalar.activation(oout[u][:, BANK * half:BANK * (half + 1)], o_ps[:], ACT.Copy).then_inc(o_copied, 1)

            groups(act, body)
            copy_o(N_GROUPS - 1, 1, 1, N_GROUPS // 2)

        @block.vector
        def _(dve):
            dve.sem_inc(nmt_ready, 1)
            dve.sem_inc(nm_stored, 16)
            dve.sem_inc(piece_maxed, BANKS + NP)

            def piece_max(n, hg, p):
                dve.wait_ge(piece_done, NP * n + p + 1)
                row_max(nc, mx[hg % 2], piece_ps(p), PIECES[p]).then_inc(piece_maxed, 1)

            def negate_step(n, hg, step):
                u = hg % 2
                m = mx[u][:, 0, :, :].rearrange("p h t -> p (h t)")
                if step == 0:
                    dve.wait_ge(piece_maxed, NP * (n + 1) + BANKS)
                    nc.vector.tensor_tensor(mx[u][:, 0, :, QT // 2:QT], mx[u][:, 0, :, QT // 2:QT],
                                            mx[u][:, 1, :, QT // 2:QT], ALU.max).then_inc(m_chain, 1)
                    return
                dve.wait_ge(m_chain, (CHAIN - 1) * n + step)
                if step == 1:
                    dve.wait_ge(nmt_done, n + 1)
                    nc.vector.tensor_scalar(nm[:, 0, :], m, -1.0, None, ALU.mult).then_inc(m_chain, 1)
                elif step == 2:
                    nc.vector.scalar_tensor_tensor(rest[:], m, -1.0, nm[:, 0, :], ALU.mult, ALU.subtract).then_inc(m_chain, 1)
                elif step == 3:
                    nc.vector.tensor_copy(nm[:, 1, :], rest[:]).then_inc(m_chain, 1)
                else:
                    nc.vector.tensor_tensor(nm[:, 2, :], rest[:], nm[:, 1, :], ALU.subtract).then_inc(nm_ready, 1)

            def copy_turned(n, hg):
                dve.wait_ge(nmt_done, n + 2)
                dve.wait_ge(nm_stored, 16 * PARTS * n + 16)
                nc.vector.tensor_copy(nmt[:], turned).then_inc(nmt_ready, 1)

            def early(n, hg, more):
                for p in range(EARLY):
                    if p == TURN:
                        copy_turned(n, hg)
                    if more:
                        piece_max(n + 1, hg + 1, p)
                    if p < CHAIN:
                        negate_step(n, hg, p)

            for step in range(CHAIN):
                negate_step(0, 0, step)
            copy_turned(0, 0)
            for p in range(EARLY):
                piece_max(1, 1, p)

            def body(bt, hg, before, follow):
                if follow:
                    n = HG * bt + hg
                    for p in range(EARLY, NP):
                        piece_max(n + 1, hg + 1, p)
                    early(n + 1, hg + 1, follow == 2)

            groups(dve, body)

        @block.tensor
        def _(pe):
            pe.sem_inc(av_done, BUFS)
            pe.sem_inc(nmt_done, 1)
            pe.sem_inc(piece_done, NP)

            def piece(n, hg, p):
                if p == TURN + BANKS - 1:
                    pe.wait_ge(nmt_ready, n + 1)
                pe.wait_ge(piece_maxed, NP * n + p + (2 if TURN <= p < TURN + BANKS - 1 else 1))
                piece_products(nc, piece_ps(p), qs[hg % HG], ks[hg % HG], PIECES[p], keep).then_inc(piece_done, 1)

            def transpose_max(n, hg, more):
                pe.wait_ge(nm_ready, n + 1)
                if more:
                    pe.wait_ge(piece_maxed, NP * (n + 1) + TURN + 1)
                nc.tensor.transpose(turned, nm[:].rearrange("p a m -> p (a m)"), identb[:]).then_inc(nmt_done, 1)

            def search(bt, hg, p, follow):
                n = HG * bt + hg
                if p < NP:
                    piece(n + 1, hg + 1, p)
                    return
                if p - NP == TURN:
                    transpose_max(n + 1, hg + 1, follow == 2)
                if follow == 2:
                    if p == NP:
                        pe.wait_ge(qk_loaded[(hg + 2) % HG], LOADS * 16 * (bt + (hg + 2) // HG + 1))
                    piece(n + 2, hg + 2, p - NP)

            transpose_max(0, 0, False)
            pe.wait_ge(nmt_ready, 2)
            for hg in range(2):
                pe.wait_ge(qk_loaded[hg], LOADS * 16)
            for p in range(EARLY):
                piece(1, 1, p)
            pe.wait_ge(k_ones, 16 * HG)

            def body(bt, hg, before, follow):
                n = HG * bt + hg
                turns = range(EARLY, NP + EARLY)
                turn = 0
                now = dve_free = act_free = 0
                bank_free, unit_free = [0] * BANKS, [0, 0]

                def pace(cols):
                    nonlocal now, turn, dve_free
                    now += cols
                    while follow and turn < len(turns) and bank_free[0] <= now:
                        p = turns[turn]
                        search(bt, hg, p, follow)
                        qt, half, _, heads, keys = PIECES[p % NP]
                        now += heads * (keys + (P if qt // HG == half else 0)) + (P if p == NP + TURN else 0)
                        dve_free = max(dve_free, now + TO_OTHER) + DVE_COLUMN * heads * keys + DVE_START
                        if NP <= p < NP + CHAIN or p == NP + TURN:
                            dve_free += DVE_START + P
                        bank_free[:] = *bank_free[1:], dve_free + TO_TENSOR
                        turn += 1

                def scores(unit):
                    nonlocal now, act_free
                    step, first, heads = UNITS[unit]
                    _, kt, lo, hi = STEPS[step]
                    while now < unit_free[0]:
                        pace(P)
                    if unit == 0:
                        pe.wait_ge(nm_stored, 16 * PARTS * (n + 1) + 16)
                    pe.wait_ge(exp_done, NU * n + unit + 1)
                    for j in range(heads):
                        i = nc.tensor.matmul(unit_ps(unit)[:, j, :], ks[hg][0:ROWS, first + j, kt * P:(kt + 1) * P],
                                             qs[hg][0:ROWS, first + j, lo:hi], start=True, stop=True)
                        if j == heads - 1:
                            i.then_inc(st_done, 1)
                        pace(hi - lo)
                    act_free = max(act_free, now + TO_OTHER) + ACT_COLUMN * heads * (hi - lo) + ACT_START
                    unit_free[:] = unit_free[1], act_free + TO_TENSOR

                def values(n, step, u):
                    half, kt, lo, hi = STEPS[step]
                    if kt // HG == half:
                        pe.wait_ge(masked, QT * n + kt + 2)
                    else:
                        pe.wait_ge(exp_done, NU * n + LAST_OF[step] + 3)
                    if kt == 0:
                        pe.wait_ge(v_ready, n + 1)
                        pe.wait_ge(o_copied, 2 * n + half + 1)
                    for j in range(HG):
                        i = nc.tensor.matmul(o_ps[2 * HD * j:2 * HD * (j + 1), lo - BANK * half:BANK], va[u][:, kt, j, :],
                                             prob[step % BUFS][:, j, 0:hi - lo], start=(kt == 0), stop=(P * (kt + 1) == hi))
                    i.then_inc(av_done, 1)
                    pace(HG * (hi - lo) + P)

                for unit, (step, first, heads) in enumerate(UNITS):
                    scores(unit)
                    for due in range(NS):
                        if DUE[due] == unit + NU and before:
                            values(n - 1, due, (hg + 1) % 2)
                        if DUE[due] == unit:
                            values(n, due, hg % 2)
                if not follow:
                    for due in range(NS):
                        if DUE[due] >= NU:
                            values(n, due, hg % 2)
                pace(float("inf"))

            groups(pe, body)


def load_pair(sp, od, keep, i, c):
    sp.dma_start(keep["ot"][c][:], od[:, :, :, bass.ds(P * i, 2 * P)].rearrange("h j r n -> (j r) h n")).then_inc(keep["ot_loaded"][c], 16)


def combine(nc, out, scratch, keep):
    od, ident = scratch["o"], keep["ident"]
    N = TOK // P
    S = 2 * OT
    R = HD + 1
    with ExitStack() as ctx:
        b = Bufs(nc, ctx)
        wo_raw, w_loaded = keep["wo"], keep["wo_loaded"]
        ot, loaded = keep["ot"], keep["ot_loaded"]
        woh = b.sb("c_woh", [P, HALVES, DIM], F32R)
        wol = b.sb("c_wol", [P, HALVES, DIM], F32R)
        gate = [b.sb(f"c_gate{s}", [P, DIM]) for s in range(S)]
        inv = [b.sb(f"c_inv{s}", [P, HEADS, 1]) for s in range(S)]
        on = [b.sb(f"c_on{s}", [P, HEADS, HD]) for s in range(S)]
        onh = [b.sb(f"c_onh{s}", [P, HALVES, P], F32R) for s in range(S)]
        onl = [b.sb(f"c_onl{s}", [P, HALVES, P], F32R) for s in range(S)]
        res = [b.sb(f"c_res{c}", [P, 2, DIM]) for c in range(S // 2)]
        t_ps = [b.ps(f"c_t_ps{u}", [P, HEADS, R]) for u in range(2)]
        b_ps = [b.ps(f"c_b_ps{u}", [P, HALVES, P]) for u in range(2)]
        s_ps = [b.ps(f"c_s_ps{u}", [P, DIM]) for u in range(2)]

        w_high, w_split = b.sem("c_w_high"), b.sem("c_w_split")
        heads_done, inv_done, divided, back_done = b.sem("c_heads_done"), b.sem("c_inv_done"), b.sem("c_divided"), b.sem("c_back_done")
        high_done, low_done, proj_done = b.sem("c_high_done"), b.sem("c_low_done"), b.sem("c_proj_done")
        gated, mixed, added = b.sem("c_gated"), b.sem("c_mixed"), b.sem("c_added")
        stored = [b.sem(f"c_stored{c}") for c in range(S // 2)]

        block = ctx.enter_context(nc.Block())

        def steps(eng, lags, body):
            deepest = max(lags)

            def step(q, r):
                for k, lag in enumerate(lags):
                    i = S * q + r - lag
                    if isinstance(q, int) and not 0 <= i < N:
                        continue
                    body(k, i, (r - lag) % S, q + 1 + (r - lag) // S)

            assert deepest <= S
            for r in range(S):
                step(0, r)
            with eng.Fori(1, N // S) as q:
                for r in range(S):
                    step(q, r)
            for r in range(deepest):
                step(N // S, r)

        @block.sync
        def _(sp):
            def body(k, i, s, nth):
                c = s // 2
                if k == 0 and s % 2 == 0 and not (isinstance(i, int) and i < S):
                    sp.wait_ge(added, i + 2)
                    load_pair(sp, od, keep, i, c)
                if k == 1 and s % 2 == 1:
                    sp.wait_ge(added, i + S + 1)
                    sp.dma_start(out[bass.ds(P * i - P, 2 * P), :].rearrange("(t p) d -> p t d", p=P), res[c][:]).then_inc(stored[c], 16)

            steps(sp, (0, S - 1), body)
            for c in range(S // 2):
                sp.wait_ge(stored[c], 16 * (N // S + 1))

        @block.gpsimd
        def _(pool):
            pool.sem_inc(added, S)

            def body(k, i, s, nth):
                pool.wait_ge(mixed, i + S + 1)
                c, t = s // 2, s % 2
                nc.gpsimd.tensor_tensor(res[c][:, t, :], res[c][:, t, :],
                                        keep["x"][:, bass.ds(i, 1), :].squeeze(1), ALU.add).then_inc(added, 1)

            steps(pool, (0,), body)

        @block.scalar
        def _(act):
            act.preload_act_table(ACT.Silu)
            for c in range(S // 2):
                act.sem_inc(stored[c], 16)

            def body(k, i, s, nth):
                if k == 0:
                    act.wait_ge(mixed, i + 1)
                    nc.scalar.activation(gate[s][:], keep["f"][:, bass.ds(i, 1), :].squeeze(1), ACT.Silu).then_inc(gated, 1)
                else:
                    act.wait_ge(back_done, i + 1)
                    act.wait_ge(proj_done, i + 1)
                    nc.scalar.activation(onh[s][:], b_ps[s % 2][:], ACT.Copy).then_inc(high_done, 1)

            steps(act, (0, 1), body)

        @block.vector
        def _(dve):
            dve.sem_inc(divided, 2)
            dve.sem_inc(low_done, 2)
            dve.sem_inc(mixed, S)
            dve.wait_ge(w_loaded, 16)
            nc.vector.tensor_copy(woh[:], wo_raw[:]).then_inc(w_high, 1)
            dve.wait_ge(w_high, 1)
            nc.vector.tensor_tensor(wol[:], wo_raw[:], woh[:].bitcast(F32), ALU.subtract).then_inc(w_split, 1)

            def body(k, i, s, nth):
                if k == 0:
                    dve.wait_ge(heads_done, i + 1)
                    nc.vector.reciprocal(inv[s][:], t_ps[s % 2][:, :, HD:HD + 1]).then_inc(inv_done, 1)
                    dve.wait_ge(inv_done, i + 1)
                    nc.vector.tensor_tensor(on[s][:], t_ps[s % 2][:, :, 0:HD], inv[s][:].broadcast_to([P, HEADS, HD]),
                                            ALU.mult).then_inc(divided, 1)
                elif k == 1:
                    dve.wait_ge(high_done, i + 1)
                    nc.vector.tensor_tensor(onl[s][:], b_ps[s % 2][:], onh[s][:].bitcast(F32), ALU.subtract).then_inc(low_done, 1)
                else:
                    dve.wait_ge(proj_done, i + S + 1)
                    dve.wait_ge(gated, i + 1)
                    dve.wait_ge(stored[s // 2], 16 * nth)
                    nc.vector.tensor_tensor(res[s // 2][:, s % 2, :], s_ps[s % 2][:], gate[s][:], ALU.mult).then_inc(mixed, 1)

            steps(dve, (0, 1, 2), body)

        @block.tensor
        def _(pe):
            pe.sem_inc(proj_done, S)
            pe.wait_ge(w_split, 1)

            def body(k, i, s, nth):
                u = s % 2
                if k == 0:
                    pe.wait_ge(loaded[s // 2], 16 * nth)
                    pe.wait_ge(divided, i + 1)
                    for h in range(HG):
                        n = nc.tensor.transpose(t_ps[u][:, h * HG:(h + 1) * HG, :], ot[s // 2][:, h, s % 2 * P:(s % 2 + 1) * P],
                                                ident[0:HG * R, 0:HG * R])
                    n.then_inc(heads_done, 1)
                elif k == 1:
                    pe.wait_ge(divided, i + 3)
                    pe.wait_ge(low_done, i + 1)
                    for c in range(HALVES):
                        n = nc.tensor.transpose(b_ps[u][:, c, :], on[s][:, c * P // HD:(c + 1) * P // HD, :].rearrange("p h d -> p (h d)"), ident[:])
                    n.then_inc(back_done, 1)
                else:
                    pe.wait_ge(low_done, i + 3)
                    pe.wait_ge(mixed, i + S - 1)
                    for c in range(HALVES):
                        for t, w in ((onh, woh), (onh, wol), (onl, woh)):
                            n = nc.tensor.matmul(s_ps[u][:], t[s][:, c, :], w[:, c, :],
                                                 start=(c == 0 and t is onh and w is woh), stop=(c == HALVES - 1 and t is onl))
                    n.then_inc(proj_done, 1)

            steps(pe, (0, 1, 2), body)


def gated_block(nc, x, wqkv, wout, w1t, b1, w2t, b2, ln_g, ln_b, out):
    scratch = {
        "q": nc.dram_tensor("q_parts", [DIM, PARTS, TOK], BF16, kind="Internal").ap(),
        "k": nc.dram_tensor("k_parts", [DIM, PARTS, TOK], BF16, kind="Internal").ap(),
        "v": nc.dram_tensor("values", [TOK, DIM], F32, kind="Internal").ap(),
        "f": nc.dram_tensor("mlp_out", [TOK, DIM], F32, kind="Internal").ap(),
        "o": nc.dram_tensor("attention_t", [HG, HG, HD + 1, TOK], F32, kind="Internal").ap(),
    }
    with ExitStack() as ctx:
        b = Bufs(nc, ctx)
        keep = {
            "ident": b.sb("ident", [P, P]), "mhalf": b.sb("mhalf", [P, TILES]),
            "identb": b.sb("identb", [P, P], BF16), "maskb": b.sb("maskb", [P, P], BF16),
            "shared": [b.sb(f"shared{n}", [P, HALVES * HID], F32R) for n in range(4)],
            "mx": [b.sb(f"mx{u}", [P, 2, HG, QT]) for u in range(2)],
        }
        with ExitStack() as inner:
            b = Bufs(nc, inner)
            keep |= {
                "xth": b.sb("xth", [P, HALVES, TOK], F32R),
                "xtl": b.sb("xtl", [P, HALVES, TOK], F32R),
                "xres": b.sb("xres", [P, TOK // P, DIM]),
                "y": [b.sb(f"y{u}", [P, TILES, DIM]) for u in range(2)],
            }
            project(nc, x, wqkv, scratch, keep)
            mlp(nc, w1t, w2t, b1, b2, ln_g, ln_b, scratch, keep)
        b = Bufs(nc, ctx)
        keep |= {"x": b.sb("x_rows", [P, TOK // P, DIM]), "f": b.sb("f_rows", [P, TOK // P, DIM]), "rows_loaded": b.sem("rows_loaded")}
        keep |= {
            "wo": b.sb("wo_raw", [P, HALVES, DIM]), "wo_loaded": b.sem("wo_loaded"),
            "ot": [b.sb(f"ot{c}", [HG * (HD + 1), HG, 2 * P]) for c in range(OT)],
            "ot_loaded": [b.sem(f"ot_loaded{c}") for c in range(OT)],
        }
        attend(nc, x, wout, scratch, keep)
        combine(nc, out, scratch, keep)


def kernel(L0_attn_x, L0_attn_w_qkv, L0_attn_w_out, L0_ffn_W1, L0_ffn_B1, L0_ffn_W2, L0_ffn_B2, L0_ffn_LN_G, L0_ffn_LN_B):
    import numpy as np
    import concourse.bacc as bacc
    from concourse.bass_utils import run_bass_kernel_spmd

    nc = bacc.Bacc("TRN2", target_bir_lowering=False, num_devices=1)
    arrays = {
        "x": np.asarray(L0_attn_x).reshape(TOK, DIM),
        "w_qkv": np.asarray(L0_attn_w_qkv),
        "w_out": np.asarray(L0_attn_w_out),
        "w1t": np.asarray(L0_ffn_W1).transpose(0, 2, 1),
        "b1": np.asarray(L0_ffn_B1).reshape(BLOCKS, CH, P).transpose(0, 2, 1),
        "w2t": np.asarray(L0_ffn_W2).transpose(0, 2, 1),
        "b2": np.asarray(L0_ffn_B2),
        "ln_g": np.asarray(L0_ffn_LN_G),
        "ln_b": np.asarray(L0_ffn_LN_B),
    }
    arrays = {k: np.ascontiguousarray(v) for k, v in arrays.items()}
    args = [nc.dram_tensor(k, v.shape, mybir.dt.from_np(v.dtype), kind="ExternalInput").ap() for k, v in arrays.items()]
    out = nc.dram_tensor("out", [TOK, DIM], F32, kind="ExternalOutput").ap()
    gated_block(nc, *args, out)
    r = run_bass_kernel_spmd(nc, [arrays], core_ids=[0])
    return r.results[0]["out"].reshape(BATCH, SEQ, DIM)
```
